# Optimizing a Trainium2 kernel written in Bass

```python
import numpy as np
import jax
import jax.numpy as jnp

def _softmax(x, axis=-1):
    return jax.nn.softmax(x, axis=axis)

def _gelu(x):
    return jax.nn.gelu(x, approximate=True)

def _silu(x):
    return jax.nn.silu(x)

def _sigmoid(x):
    return jax.nn.sigmoid(x)

def _layernorm(x, axis=-1, eps=1e-05):
    m = jnp.mean(x, axis=axis, keepdims=True)
    v = jnp.var(x, axis=axis, keepdims=True)
    return (x - m) / jnp.sqrt(v + eps)

def _scatter_add(tgt, idx, src, axis=0):
    return tgt.at[idx].add(src)

def _segment_sum(src, seg, n):
    return jax.ops.segment_sum(src, seg, n)
kernel_name = 'mk_adaln_ffn_d2_seqx_r4_a8d453'

def setup_inputs(seed: int=0):
    np.random.seed(seed)
    _w = jnp.asarray

    def _rec_inputs():
        import jax
        import jax.numpy as jnp
        _rk = jax.random.key(seed)
        x = -0.0002928 + 1 * jax.random.normal(jax.random.fold_in(_rk, 1), (16, 256, 256), jnp.float32)
        _lenS = 256 - jax.random.randint(jax.random.fold_in(_rk, 7), (16,), 0, max(1, 256 // 4) + 1, jnp.int32)
        _lenS2 = 256 - jax.random.randint(jax.random.fold_in(_rk, 8), (16,), 0, max(1, 256 // 4) + 1, jnp.int32)
        cond_1024 = 0.0061147 + 1.02565 * jax.random.normal(jax.random.fold_in(_rk, 11), (16, 256), jnp.float32)
        return (x, cond_1024)
    x, cond_1024 = _rec_inputs()

    def _L0_cond_setup():
        import jax, jax.numpy as jnp
        import numpy as np
        D, HS, HE, E, K = (256, 512, 256, 8, 2)
        B, T = (4, 256)
        N_SHARED = 1
        key = jax.random.key(seed)
        ks = jax.random.split(key, 9)
        g = lambda k, shape, s: jax.random.normal(k, shape, jnp.float32) * s
        return {'x': g(ks[0], (B, T, D), 1.0), 't_emb': g(ks[1], (B, D), 1.0), 'router_W': g(ks[2], (2 * D, E), 0.01), 'router_bias': jnp.zeros((E,), jnp.float32), 'w1': g(ks[3], (D, HS), 0.02), 'w3': g(ks[4], (D, HS), 0.02), 'w2': g(ks[5], (HS, D), 0.02), 'W1e': g(ks[6], (E, D, HE), 0.02), 'W2e': g(ks[7], (E, HE, D), 0.02)}
    _L0_cond_all = _L0_cond_setup()
    _L0_cond_in = {k: v for k, v in _L0_cond_all.items() if k in ('router_W', 'router_bias', 'w1', 'w3', 'w2', 'W1e', 'W2e')}
    del _L0_cond_all

    def _L0_ffn_setup():
        import jax, jax.numpy as jnp
        import numpy as np
        TOPK = 8
        BN_EPS = 1e-05
        key = jax.random.key(seed)
        ks = jax.random.split(key, 5)
        b, n, d = (2, 256, 256)
        h, nk, kd = (8, 64, 128)
        ne = nk * nk
        scale = 0.02
        return {'inputs': jax.random.normal(ks[0], (b, n, d), jnp.float32), 'gamma': jnp.ones((d,), jnp.float32), 'beta': jnp.zeros((d,), jnp.float32), 'w_q': jax.random.normal(ks[1], (2 * h * kd, d), jnp.float32) * scale, 'keys': jax.random.normal(ks[2], (h, nk, 2, kd), jnp.float32) * scale, 'key_in': jax.random.normal(ks[3], (ne, d), jnp.float32) * scale, 'key_out': jax.random.normal(ks[4], (ne, d), jnp.float32) * scale}
    _L0_ffn_all = _L0_ffn_setup()
    _L0_ffn_in = {k: v for k, v in _L0_ffn_all.items() if k in ('gamma', 'beta', 'w_q', 'keys', 'key_in', 'key_out')}
    del _L0_ffn_all

    def _L1_cond_setup():
        import jax, jax.numpy as jnp
        import numpy as np
        import math
        D = 256
        H = 256
        key = jax.random.key(seed)
        k1, k2, k3, k4 = jax.random.split(key, 4)
        x = jax.random.normal(k1, (64, 128, D), dtype=jnp.float32)
        h0 = jax.random.normal(k2, (64, H), dtype=jnp.float32)
        Wx = jax.random.normal(k3, (D, 4 * H), dtype=jnp.float32) / math.sqrt(D)
        Wh = jax.random.normal(k4, (H, 4 * H), dtype=jnp.float32) / math.sqrt(H)
        b = jnp.zeros((4 * H,), dtype=jnp.float32)
        return {'x': x, 'h0': h0, 'Wx': Wx, 'Wh': Wh, 'b': b}
    _L1_cond_all = _L1_cond_setup()
    _L1_cond_in = {k: v for k, v in _L1_cond_all.items() if k in ('Wx', 'Wh', 'b')}
    del _L1_cond_all

    def _L1_ffn_setup():
        import jax, jax.numpy as jnp
        import numpy as np
        D = 256
        H = 16
        DK = D // H
        E = 8
        DFF = 4 * D
        TOPK = 2
        EPS = 1e-05

        def _layernorm(x, g, b):
            m = jnp.mean(x, axis=-1, keepdims=True)
            v = jnp.mean(jnp.square(x - m), axis=-1, keepdims=True)
            return (x - m) * jax.lax.rsqrt(v + EPS) * g + b
        key = jax.random.key(seed)
        ks = jax.random.split(key, 16)
        s_in = 1.0 / np.sqrt(D)
        s_ff = 1.0 / np.sqrt(DFF)
        return {'x': jax.random.normal(ks[0], (2, 512, D), dtype=jnp.float32), 'ln1_g': jnp.ones((D,), jnp.float32), 'ln1_b': jnp.zeros((D,), jnp.float32), 'w_qkv': jax.random.normal(ks[1], (D, 3 * D), jnp.float32) * s_in, 'b_qkv': jnp.zeros((3 * D,), jnp.float32), 'w_o': jax.random.normal(ks[2], (D, D), jnp.float32) * s_in, 'b_o': jnp.zeros((D,), jnp.float32), 'ln2_g': jnp.ones((D,), jnp.float32), 'ln2_b': jnp.zeros((D,), jnp.float32), 'gate_w': jax.random.normal(ks[3], (D, E), jnp.float32) * s_in, 'gate_b': jnp.zeros((E,), jnp.float32), 'W1': jax.random.normal(ks[4], (E, D, DFF), jnp.float32) * s_in, 'b1': jnp.zeros((E, DFF), jnp.float32), 'W2': jax.random.normal(ks[5], (E, DFF, D), jnp.float32) * s_ff, 'b2': jnp.zeros((E, D), jnp.float32)}
    _L1_ffn_all = _L1_ffn_setup()
    _L1_ffn_in = {k: v for k, v in _L1_ffn_all.items() if k in ('ln1_g', 'ln1_b', 'w_qkv', 'b_qkv', 'w_o', 'b_o', 'ln2_g', 'ln2_b', 'gate_w', 'gate_b', 'W1', 'b1', 'W2', 'b2')}
    del _L1_ffn_all
    return {'x': x, 'cond_1024': cond_1024, 'L0_cond_router_W': _L0_cond_in['router_W'], 'L0_cond_router_bias': _L0_cond_in['router_bias'], 'L0_cond_w1': _L0_cond_in['w1'], 'L0_cond_w3': _L0_cond_in['w3'], 'L0_cond_w2': _L0_cond_in['w2'], 'L0_cond_W1e': _L0_cond_in['W1e'], 'L0_cond_W2e': _L0_cond_in['W2e'], 'L0_ffn_gamma': _L0_ffn_in['gamma'], 'L0_ffn_beta': _L0_ffn_in['beta'], 'L0_ffn_w_q': _L0_ffn_in['w_q'], 'L0_ffn_keys': _L0_ffn_in['keys'], 'L0_ffn_key_in': _L0_ffn_in['key_in'], 'L0_ffn_key_out': _L0_ffn_in['key_out'], 'L1_cond_Wx': _L1_cond_in['Wx'], 'L1_cond_Wh': _L1_cond_in['Wh'], 'L1_cond_b': _L1_cond_in['b'], 'L1_ffn_ln1_g': _L1_ffn_in['ln1_g'], 'L1_ffn_ln1_b': _L1_ffn_in['ln1_b'], 'L1_ffn_w_qkv': _L1_ffn_in['w_qkv'], 'L1_ffn_b_qkv': _L1_ffn_in['b_qkv'], 'L1_ffn_w_o': _L1_ffn_in['w_o'], 'L1_ffn_b_o': _L1_ffn_in['b_o'], 'L1_ffn_ln2_g': _L1_ffn_in['ln2_g'], 'L1_ffn_ln2_b': _L1_ffn_in['ln2_b'], 'L1_ffn_gate_w': _L1_ffn_in['gate_w'], 'L1_ffn_gate_b': _L1_ffn_in['gate_b'], 'L1_ffn_W1': _L1_ffn_in['W1'], 'L1_ffn_b1': _L1_ffn_in['b1'], 'L1_ffn_W2': _L1_ffn_in['W2'], 'L1_ffn_b2': _L1_ffn_in['b2']}

def reference(x, cond_1024, L0_cond_router_W, L0_cond_router_bias, L0_cond_w1, L0_cond_w3, L0_cond_w2, L0_cond_W1e, L0_cond_W2e, L0_ffn_gamma, L0_ffn_beta, L0_ffn_w_q, L0_ffn_keys, L0_ffn_key_in, L0_ffn_key_out, L1_cond_Wx, L1_cond_Wh, L1_cond_b, L1_ffn_ln1_g, L1_ffn_ln1_b, L1_ffn_w_qkv, L1_ffn_b_qkv, L1_ffn_w_o, L1_ffn_b_o, L1_ffn_ln2_g, L1_ffn_ln2_b, L1_ffn_gate_w, L1_ffn_gate_b, L1_ffn_W1, L1_ffn_b1, L1_ffn_W2, L1_ffn_b2):
    import jax
    import jax.numpy as jnp

    def _L0_cond_ref(x, t_emb, router_W, router_bias, w1, w3, w2, W1e, W2e):
        import jax, jax.numpy as jnp
        import numpy as np
        D, HS, HE, E, K = (256, 512, 256, 8, 2)
        B, T = (4, 256)
        N_SHARED = 1
        Bb, Tt, C = x.shape
        xf = x.reshape(-1, C)
        tf = jnp.broadcast_to(t_emb[:, None, :], (Bb, Tt, C)).reshape(-1, C)
        N = xf.shape[0]
        shared = jax.nn.silu(xf @ w1) * (xf @ w3) @ w2
        s = jax.nn.sigmoid((jnp.concatenate([xf, tf], axis=-1) @ router_W).astype(jnp.float32))
        sel_scores = s + router_bias
        _, topk_idx = jax.lax.top_k(sel_scores, K)
        s_sel = jnp.take_along_axis(s, topk_idx, axis=1)
        denom = s_sel.sum(axis=1, keepdims=True)
        gates = jnp.where(denom > 1e-09, s_sel / (denom + 1e-09), 1.0 / K).astype(x.dtype)
        combine = jnp.zeros((N, E), x.dtype).at[jnp.arange(N)[:, None], topk_idx].add(gates)
        h = jax.nn.gelu(jnp.einsum('nc,ech->enh', xf, W1e), approximate=False)
        y = jnp.einsum('enh,ehc->enc', h, W2e)
        routed = jnp.einsum('ne,enc->nc', combine, y)
        return ((shared + routed) / (N_SHARED + K)).reshape(Bb, Tt, C)

    def _L0_ffn_ref(inputs, gamma, beta, w_q, keys, key_in, key_out):
        import jax, jax.numpy as jnp
        import numpy as np
        TOPK = 8
        BN_EPS = 1e-05
        b, n, d = inputs.shape
        h, nk, _, kd = keys.shape
        k = TOPK
        x = inputs.reshape(b * n, d)
        mu = jnp.mean(x, axis=0)
        var = jnp.mean(jnp.square(x - mu), axis=0)
        xn = (x - mu) * jax.lax.rsqrt(var + BN_EPS) * gamma + beta
        q = (xn @ w_q.T).reshape(b, n, 2, h, kd).transpose(2, 0, 1, 3, 4)
        sim = jnp.einsum('pbnhd,hkpd->pbnhk', q, keys)
        s, i = jax.lax.top_k(sim, k)
        sx, sy = (s[0], s[1])
        ix, iy = (i[0], i[1])
        all_scores = (sx[..., :, None] + sy[..., None, :]).reshape(b, n, h, k * k)
        all_idx = (ix[..., :, None] * nk + iy[..., None, :]).reshape(b, n, h, k * k)
        scores, pk = jax.lax.top_k(all_scores, k)
        idx = jnp.take_along_axis(all_idx, pk, axis=-1)
        w_down = key_in[idx]
        w_up = key_out[idx]
        o = jnp.einsum('bnd,bnhkd->bnhk', inputs, w_down)
        o = jax.nn.gelu(o, approximate=False) * jax.nn.softmax(scores, axis=-1)
        return jnp.einsum('bnhk,bnhkd->bnd', o, w_up)

    def _L1_cond_ref(x, h0, Wx, Wh, b):
        import jax, jax.numpy as jnp
        import numpy as np
        import math
        D = 256
        H = 256
        Hdim = h0.shape[1]
        xW = jnp.einsum('ntd,dk->ntk', x, Wx) + b
        c0 = jnp.zeros_like(h0)

        def step(carry, xw_t):
            prev_h, prev_c = carry
            a = xw_t + prev_h @ Wh
            i = jax.nn.sigmoid(a[:, :Hdim])
            f = jax.nn.sigmoid(a[:, Hdim:2 * Hdim])
            o = jax.nn.sigmoid(a[:, 2 * Hdim:3 * Hdim])
            g = jnp.tanh(a[:, 3 * Hdim:])
            next_c = f * prev_c + i * g
            next_h = o * jnp.tanh(next_c)
            return ((next_h, next_c), next_h)
        xW_t = jnp.swapaxes(xW, 0, 1)
        _, hs = jax.lax.scan(step, (h0, c0), xW_t)
        hn = jnp.swapaxes(hs, 0, 1)
        return hn

    def _L1_ffn_ref(x, ln1_g, ln1_b, w_qkv, b_qkv, w_o, b_o, ln2_g, ln2_b, gate_w, gate_b, W1, b1, W2, b2):
        import jax, jax.numpy as jnp
        import numpy as np
        D = 256
        H = 16
        DK = D // H
        E = 8
        DFF = 4 * D
        TOPK = 2
        EPS = 1e-05

        def _layernorm(x, g, b):
            m = jnp.mean(x, axis=-1, keepdims=True)
            v = jnp.mean(jnp.square(x - m), axis=-1, keepdims=True)
            return (x - m) * jax.lax.rsqrt(v + EPS) * g + b
        B, S, _ = x.shape
        h = _layernorm(x, ln1_g, ln1_b)
        qkv = h @ w_qkv + b_qkv
        q, k, v = jnp.split(qkv, 3, axis=-1)
        q = q.reshape(B, S, H, DK)
        k = k.reshape(B, S, H, DK)
        v = v.reshape(B, S, H, DK)
        scores = jnp.einsum('bqhd,bkhd->bhqk', q, k) / np.sqrt(DK)
        attn = jax.nn.softmax(scores, axis=-1)
        o = jnp.einsum('bhqk,bkhd->bqhd', attn, v).reshape(B, S, D)
        x = x + o @ w_o + b_o
        h = _layernorm(x, ln2_g, ln2_b).reshape(B * S, D)
        logits = h @ gate_w + gate_b
        topv, topi = jax.lax.top_k(logits, TOPK)
        gw = jax.nn.softmax(topv, axis=-1)
        ew = jnp.sum(jax.nn.one_hot(topi, E, dtype=h.dtype) * gw[..., None], axis=1)
        hid = jax.nn.relu(jnp.einsum('td,edf->etf', h, W1) + b1[:, None, :])
        out_e = jnp.einsum('etf,efd->etd', hid, W2) + b2[:, None, :]
        moe = jnp.einsum('etd,te->td', out_e, ew)
        return x + moe.reshape(B, S, D)
    x = x + _L0_ffn_ref(_L0_cond_ref(x, cond_1024, L0_cond_router_W, L0_cond_router_bias, L0_cond_w1, L0_cond_w3, L0_cond_w2, L0_cond_W1e, L0_cond_W2e), L0_ffn_gamma, L0_ffn_beta, L0_ffn_w_q, L0_ffn_keys, L0_ffn_key_in, L0_ffn_key_out)
    x = x + _L1_ffn_ref(_L1_cond_ref(x, cond_1024, L1_cond_Wx, L1_cond_Wh, L1_cond_b), L1_ffn_ln1_g, L1_ffn_ln1_b, L1_ffn_w_qkv, L1_ffn_b_qkv, L1_ffn_w_o, L1_ffn_b_o, L1_ffn_ln2_g, L1_ffn_ln2_b, L1_ffn_gate_w, L1_ffn_gate_b, L1_ffn_W1, L1_ffn_b1, L1_ffn_W2, L1_ffn_b2)
    return x

_drawn_inputs = setup_inputs


def setup_inputs(seed=0):
    import zlib

    import numpy as np

    out = dict(_drawn_inputs(seed))
    spreads = {'L0_cond_router_bias': (0.0, 0.8),
     'L0_ffn_gamma': (1.0, 0.6),
     'L0_ffn_beta': (0.0, 0.8),
     'L1_cond_b': (0.0, 0.1),
     'L1_ffn_ln1_g': (1.0, 0.2),
     'L1_ffn_ln1_b': (0.0, 0.1),
     'L1_ffn_b_qkv': (0.0, 0.1),
     'L1_ffn_b_o': (0.0, 0.1),
     'L1_ffn_ln2_g': (1.0, 0.2),
     'L1_ffn_ln2_b': (0.0, 0.1),
     'L1_ffn_gate_b': (0.0, 0.1),
     'L1_ffn_b1': (0.0, 0.525),
     'L1_ffn_b2': (0.0, 0.369)}
    factors = {'L0_cond_router_W': 8.0,
     'L0_cond_w1': 8.0,
     'L0_cond_w3': 8.0,
     'L0_cond_w2': 8.0,
     'L0_cond_W1e': 8.0,
     'L0_cond_W2e': 8.0,
     'L0_ffn_w_q': 8.0,
     'L0_ffn_keys': 8.0,
     'L0_ffn_key_in': 8.0,
     'L0_ffn_key_out': 8.0}
    for name, (base, spread) in spreads.items():
        noise = np.random.default_rng([zlib.crc32(name.encode()), seed]).standard_normal(out[name].shape)
        drawn = base * np.exp(spread * noise) if base else spread * noise
        out[name] = jnp.asarray(drawn.astype(out[name].dtype))
    for name, factor in factors.items():
        out[name] = (out[name] * factor).astype(out[name].dtype)
    return out
```

```python
import concourse.bass as bass
from concourse import mybir
from contextlib import ExitStack

NB, T, D = 16, 256, 256
N = NB * T


class Program:

    def __init__(self, nc, ctx):
        self.nc, self.ctx = nc, ctx
        self.q = {k: [] for k in ("tensor", "vector", "scalar", "gpsimd", "sync")}
        self.sem = {k: ctx.enter_context(nc.semaphore("s_" + k)) for k in self.q}
        self.count = {k: 0 for k in self.q}
        self.seen = {k: {} for k in self.q}
        self.nsem = 0
        self.dma_count = {}

    def wait(self, eng, after):
        for tok in after:
            if tok is None:
                continue
            sem, v = tok
            if self.seen[eng].get(id(sem), 0) < v:
                self.seen[eng][id(sem)] = v
                self.q[eng].append(lambda e, sem=sem, v=v: e.wait_ge(sem, v))

    def op(self, eng, f, *after, sig=True):
        self.wait(eng, after)
        if not sig:
            self.q[eng].append(f)
            return None
        self.count[eng] += 1
        s = self.sem[eng]
        self.q[eng].append(lambda e: f(e).then_inc(s, 1))
        return (s, self.count[eng])

    def new_sem(self, name):
        s = self.ctx.enter_context(self.nc.semaphore(name))
        self.dma_count[id(s)] = 0
        return s

    def dma(self, eng, out, in_, sem, *after):
        self.wait(eng, after)
        self.dma_count[id(sem)] += 16
        self.q[eng].append(lambda e: e.dma_start(out, in_).then_inc(sem, 16))
        return (sem, self.dma_count[id(sem)])

    def emit(self, block):
        for name in self.q:
            def body(e, items=self.q[name]):
                for f in items:
                    f(e)
            start = {"tensor": block.tensor, "vector": block.vector, "scalar": block.scalar,
                            "gpsimd": block.gpsimd, "sync": block.sync}[name]
            start(body)


class Arena:
    def __init__(self, t, words):
        self.t, self.words, self.at = t, words, 0

    def take(self, *dims, dt=None):
        n = 1
        for d in dims:
            n *= d
        half = dt is not None and mybir.dt.size(dt) == 2
        w = (n + 1) // 2 if half else n
        w = (w + 7) // 8 * 8
        v = self.t[:, self.at:self.at + w]
        self.at += w
        assert self.at <= self.words, (self.at, self.words)
        if dt is not None:
            v = v.bitcast(dt)
        v = v[:, 0:n]
        if len(dims) == 2:
            v = v.rearrange("p (a b) -> p a b", a=dims[0])
        elif len(dims) == 3:
            v = v.rearrange("p (a b c) -> p a b c", a=dims[0], b=dims[1])
        elif len(dims) == 4:
            v = v.rearrange("p (a b c d) -> p a b c d", a=dims[0], b=dims[1], c=dims[2])
        return v


def build(nc, I, out, dbg=None):
    f32, f16, u32 = mybir.dt.float32, mybir.dt.float16, mybir.dt.uint32
    ALU, ACT, AX = mybir.AluOpType, mybir.ActivationFunctionType, mybir.AxisListType
    WORDS = 52000
    ctx = ExitStack()
    with ctx:
        P = Program(nc, ctx)
        arena = Arena(ctx.enter_context(nc.sbuf_tensor("arena", [128, WORDS], f32)), WORDS)
        ps = ctx.enter_context(nc.psum_tensor("ps", [128, 4096], f32))
        x1d = nc.dram_tensor("x1_scratch", [T, NB, D], f32, kind="Internal").ap()
        op, dma = P.op, P.dma
        take = arena.take

        def bank(b, n=1):
            return ps[:, 512 * b:512 * (b + n)]

        free = [()] * 8

        def mm(o, l, r, start, stop, *after, sig=False):
            return op("tensor", lambda e: e.matmul(o, l, r, start=start, stop=stop), *after, sig=sig)

        def tr(o, i, *after, sig=False):
            return op("tensor", lambda e: e.transpose(o, i, ident), *after, sig=sig)

        def act(o, i, fn, *after, bias=0.0, scale=1.0, acc=None):
            if acc is None:
                return op("scalar", lambda e: e.activation(o, i, fn, bias=bias, scale=scale), *after)
            return op("scalar", lambda e: e.activation(o, i, fn, bias=bias, scale=scale, accum_out=acc), *after)

        def tt(o, a, b, alu, *after):
            return op("vector", lambda e: e.tensor_tensor(o, a, b, alu), *after)

        def ts(o, a, s1, s2, o0, o1, *after):
            if o1 is None:
                return op("vector", lambda e: e.tensor_scalar(o, a, s1, None, o0), *after)
            return op("vector", lambda e: e.tensor_scalar(o, a, s1, s2, o0, o1), *after)

        def stt(o, a, s, b, o0, o1, *after):
            return op("vector", lambda e: e.scalar_tensor_tensor(o, a, s, b, o0, o1), *after)

        def cp(o, i, *after):
            return op("vector", lambda e: e.tensor_copy(o, i), *after)

        def red(o, i, alu, *after, neg=False):
            return op("vector", lambda e: e.tensor_reduce(o, i, AX.X, alu, negate=neg), *after)

        def mx8(o, i, *after):
            return op("vector", lambda e: e.max(o, i), *after)

        def ix8(o, m, v, *after):
            return op("vector", lambda e: e.max_index(o, m, v), *after)

        def recip(o, i, *after):
            return op("vector", lambda e: e.reciprocal(o, i), *after)

        def load(tile, name, *after, eng="sync"):
            s = P.new_sem("l_" + name)
            return dma(eng, tile, I[name], s, *after)

        def barrier():
            toks = [(P.sem[k], P.count[k]) for k in P.q if P.count[k]]
            for k in P.q:
                P.wait(k, toks)

        ident = take(128)
        t_id = load(ident, "ident")
        iota8 = take(8)
        t_i8 = load(iota8, "iota8")
        epst = take(1)
        t_eps = op("vector", lambda e: e.memset(epst, 1e-5))
        base = arena.at

        xcT = take(2, N)
        after_a = arena.at
        xT = [take(2, 512) for _ in range(2)]
        s_xT = [P.new_sem(f"xT{i}") for i in range(2)]
        cT, rW, rb = take(2, 128), take(4, 8), take(8)
        t_r = [load(cT, "condT"), load(rW, "rW"), load(rb, "rb")]
        w1, w3, w2 = take(2, 512), take(2, 512), take(4, 256)
        t_xT = {}

        def load_x(s, *after):
            t_xT[s] = dma("sync", xT[s % 2], I["xT"][:, :, 512 * s:512 * (s + 1)], s_xT[s % 2], *after)

        load_x(0)
        t_w = [load(w1, "w1"), load(w3, "w3"), load(w2, "w2")]
        W1e, W2e = take(8, 2, 256), take(8, 2, 256)
        t_e = [load(W1e, "W1e"), load(W2e, "W2e")]
        load_x(1)
        TL = take(8)
        comb = take(4, 8)
        sg, sl, m8, oh = take(4, 8), take(4, 8), take(4, 8), take(2, 4, 8)
        i8 = take(4, 8, dt=u32)
        i8f, sel, dn, fl, rr = take(4, 8), take(2, 4, 8), take(4), take(4), take(4)
        sv = take(2, 4)
        silu_s, hs = take(512), take(4, 512)
        he = [take(2, 512) for _ in range(2)]
        acc = take(4, 256)
        st = take(2, 8, 6)

        for k in range(2):
            t = mm(bank(0)[:, 0:8], cT[:, k, :], rW[:, 2 + k, :], k == 0, k == 1, *t_r, sig=(k == 1))
        t_TL = cp(TL, bank(0)[:, 0:8], t)
        free[0] = (t_TL,)
        t_acc_read = None
        t_he = [(), ()]
        t_hs_read = None
        t_bn = None
        for s in range(8):
            x_ = xT[s % 2]
            for j in range(4):
                for k in range(2):
                    t = mm(bank(0)[:, 8 * j:8 * j + 8], x_[:, k, 128 * j:128 * j + 128], rW[:, k, :], k == 0, k == 1,
                           t_xT[s], *free[0], sig=(j == 3 and k == 1))
            lg = bank(0)[:, 0:32].rearrange("p (a b) -> p a b", a=4)
            t = tt(sl, lg, TL.unsqueeze(1).to_broadcast([128, 4, 8]), ALU.add, t, t_TL)
            free[0] = (t,)
            t_s = act(sg, sl, ACT.Sigmoid, t)
            t = tt(sl, sg, rb.unsqueeze(1).to_broadcast([128, 4, 8]), ALU.add, t_s)
            for j in range(4):
                t1 = mx8(m8[:, j, :], sl[:, j, :], t)
            for j in range(4):
                t1 = ix8(i8[:, j, :], m8[:, j, :], sl[:, j, :], t1)
            t = cp(i8f, i8, t1)
            io = iota8.unsqueeze(1).to_broadcast([128, 4, 8])
            for k in range(2):
                t1 = tt(oh[:, k], i8f[:, :, k:k + 1].to_broadcast([128, 4, 8]), io, ALU.is_equal, t, t_i8)
                t1 = tt(sel[:, k], oh[:, k], sg, ALU.mult, t1)
                t1 = red(sv[:, k], sel[:, k], ALU.add, t1)
            t = tt(dn, sv[:, 0], sv[:, 1], ALU.add, t1)
            t = ts(fl, dn, 1e-9, None, ALU.is_gt, None, t)
            t = ts(rr, dn, 1e-9, None, ALU.add, None, t)
            t = recip(rr, rr, t)
            t = tt(rr, rr, fl, ALU.mult, t)
            t = ts(fl, fl, -0.5, 0.5, ALU.mult, ALU.add, t)
            rrb = rr.unsqueeze(2).to_broadcast([128, 4, 8])
            flb = fl.unsqueeze(2).to_broadcast([128, 4, 8])
            t = tt(sel[:, 0], sel[:, 0], sel[:, 1], ALU.add, t)
            t = tt(sel[:, 0], sel[:, 0], rrb, ALU.mult, t)
            t = tt(oh[:, 0], oh[:, 0], oh[:, 1], ALU.add, t)
            t = tt(oh[:, 0], oh[:, 0], flb, ALU.mult, t)
            t_comb = tt(comb, oh[:, 0], sel[:, 0], ALU.add, t)
            for c in range(4):
                for w, b in ((w1, 2), (w3, 3)):
                    for k in range(2):
                        t = mm(bank(b), w[:, k, 128 * c:128 * c + 128], x_[:, k, :], k == 0, k == 1, t_xT[s],
                               *t_w, *free[b], sig=(k == 1))
                    if b == 2:
                        t_u = t
                t_si = act(silu_s, bank(2), ACT.Silu, t_u, t_hs_read)
                t_hs = tt(hs[:, c, :], silu_s, bank(3), ALU.mult, t_si, t)
                t_hs_read = t_hs
                free[2], free[3] = (t_si,), (t_hs,)
            for j in range(4):
                for c in range(4):
                    t = mm(bank(4 + j // 2)[:, 256 * (j % 2):256 * (j % 2) + 256], hs[:, c, 128 * j:128 * j + 128],
                           w2[:, c, :], c == 0, c == 3, t_hs, *free[4 + j // 2], sig=(c == 3))
                if j % 2:
                    b = 4 + j // 2
                    t_acc = act(acc[:, j - 1:j + 1, :], bank(b).rearrange("p (a b) -> p a b", a=2), ACT.Copy, t,
                                t_acc_read)
                    free[b] = (t_acc,)
            for e in range(8):
                h_ = he[e % 2]
                for c in range(2):
                    b = 2 + c
                    for k in range(2):
                        t = mm(bank(b), W1e[:, e, k, 128 * c:128 * c + 128], x_[:, k, :], k == 0, k == 1, t_e[0],
                               *free[b], sig=(k == 1))
                    t_h = act(h_[:, c, :], bank(b), ACT.Gelu, t, *t_he[e % 2])
                    free[b] = (t_h,)
                for j in range(4):
                    b = 4 + j
                    o = bank(b)[:, 0:256]
                    for c in range(2):
                        t = mm(o, h_[:, c, 128 * j:128 * j + 128], W2e[:, e, c, :], c == 0, c == 1, t_h, t_e[1],
                               *free[b], sig=(c == 1))
                    t_a = stt(acc[:, j, :], o, comb[:, j, e:e + 1], acc[:, j, :], ALU.mult, ALU.add, t, t_acc, t_comb)
                    free[b] = (t_a,)
                t_acc = t_a
                t_he[e % 2] = (t,)
            if s + 2 < 8:
                load_x(s + 2, t_he[0][0], t_he[1][0])
            for c in range(2):
                b = c
                for j in range(4):
                    t = tr(bank(b)[:, 128 * j:128 * j + 128], acc[:, j, 128 * c:128 * c + 128], t_acc, t_id, *free[b],
                           sig=(j == 3))
                o = xcT[:, c, 512 * s:512 * s + 512]
                t_x = act(o, bank(b), ACT.Copy, t, scale=1.0 / 3.0)
                free[b] = (t_x,)
                t_bn = op("vector", lambda e, c=c, s=s, o=o: e.bn_stats(st[:, c, s, :], o), t_x)
            t_acc_read = t
        mv0 = take(2, 2)
        for c in range(2):
            t = op("vector", lambda e, c=c: e.bn_aggr(mv0[:, c, :], st[:, c].rearrange("p a b -> p (a b)")), t_bn)
        barrier()
        arena.at = after_a
        ga = take(2)
        ba = take(2)
        gb = [load(ga, "gamma"), load(ba, "beta")]
        mv = take(2, 2)
        t = cp(mv, mv0, t)
        a_, b_ = take(2), take(2)
        t = act(a_, mv[:, :, 1], ACT.Sqrt, t, t_eps, bias=epst)
        t = recip(a_, a_, t)
        t = tt(a_, a_, ga, ALU.mult, t, *gb)
        t = tt(b_, mv[:, :, 0], a_, ALU.mult, t)
        t_ab = tt(b_, ba, b_, ALU.subtract, t)
        if dbg:
            s = P.new_sem("dbg0")
            dma("sync", dbg["xcT"], xcT, s)

        Kc = take(2, 1024)
        x1T = xcT
        mark = arena.at
        wq, kT = take(16, 256), take(16, 64)
        t_k = [load(wq, "wq"), load(kT, "keysT")]
        for c in range(2):
            for g in range(16):
                b = 2 * c + g // 8
                t = mm(bank(b)[:, 64 * (g % 8):64 * (g % 8) + 64], wq[:, g, 128 * c:128 * c + 128], kT[:, g, :],
                       True, True, *t_k, sig=(g % 8 == 7))
                if g % 8 == 7:
                    t_Kc = cp(Kc[:, c, 512 * (g // 8):512 * (g // 8) + 512], bank(b), t)
        barrier()
        arena.at = mark
        kin, kout = take(2, 32, 128), take(32, 256)
        t_kin, t_kout = load(kin, "kinT"), load(kout, "kout")
        iot = take(32, 64, dt=f16)
        t_iot = load(iot, "iota32")
        SB = 256
        G = take(32, SB)
        X = take(128, 64, dt=f16)
        Y = take(32, 64, dt=f16)
        Y12 = take(2, 32, 64, dt=f16)
        xn = take(2, 128)
        S8, I8, I8f = take(16, 8), take(16, 8, dt=u32), take(16, 8)
        pr = take(8, 8, 8)
        sc, pk = take(8, 8), take(8, 8, dt=u32)
        ab, abf = take(2, 64, dt=u32), take(2, 64)
        eq = take(64, 8)
        ixy = take(2, 64)
        ge, es, ss = take(64), take(8, 8), take(8)
        Z = take(3, 2, 64)
        R3 = take(3, 64)
        xh16 = take(4, 64, dt=f16)
        xl16, wv = take(64, dt=f16), take(2, 64, dt=f16)
        xr = take(2, 256)
        x1 = take(2, 256)
        s_xr = [P.new_sem(f"xr{i}") for i in range(2)]
        s_x1 = [P.new_sem(f"x1{i}") for i in range(2)]
        t_xr_read = [None, None]
        t_st = [None, None]
        barrier()
        free = [()] * 8
        t_Gread = None
        t_A = {}
        for sb in range(N // SB):
            for jp in range(16):
                b = 2 + jp % 2
                for i in range(2):
                    for k in range(2):
                        t = mm(bank(b)[:, SB * i:SB * i + SB], kin[:, k, 2 * jp + i, :], xcT[:, k, SB * sb:SB * sb + SB],
                               k == 0, k == 1, t_kin, *free[b], sig=(i == 1 and k == 1))
                t_G = act(G[:, 2 * jp:2 * jp + 2, :], bank(b).rearrange("p (a b) -> p a b", a=2), ACT.Gelu, t, t_Gread)
                free[b] = (t_G,)
            for bb in range(2):
                blk = 2 * sb + bb
                n0 = 128 * blk
                t_xr = dma("sync", xr[:, bb, :], I["xtb"][blk], s_xr[bb], t_xr_read[bb])
                for c in range(2):
                    t_xn = act(xn[:, c, :], xcT[:, c, n0:n0 + 128], ACT.Identity, t_ab, *free[0], bias=b_[:, c:c + 1],
                               scale=a_[:, c:c + 1])
                for h in range(2):
                    for k in range(2):
                        t = mm(bank(h), xn[:, k, :], Kc[:, k, 512 * h:512 * h + 512], k == 0, k == 1, t_xn, t_Kc,
                               *free[h], sig=True)
                for g in range(16):
                    v = ps[:, 64 * g:64 * g + 64]
                    t1 = mx8(S8[:, g, :], v, t)
                for g in range(16):
                    v = ps[:, 64 * g:64 * g + 64]
                    t1 = ix8(I8[:, g, :], S8[:, g, :], v, t1)
                free[0] = free[1] = (t1,)
                t = cp(I8f, I8, t1)
                t1 = tt(pr, S8[:, 0:8, :].unsqueeze(3).to_broadcast([128, 8, 8, 8]),
                        S8[:, 8:16, :].unsqueeze(2).to_broadcast([128, 8, 8, 8]), ALU.add, t)
                prf = pr.rearrange("p a b c -> p a (b c)")
                for h in range(8):
                    t1 = mx8(sc[:, h, :], prf[:, h, :], t1)
                t2 = t1
                for h in range(8):
                    t1 = ix8(pk[:, h, :], sc[:, h, :], prf[:, h, :], t2)
                t = tt(es, sc, sc[:, :, 0:1].to_broadcast([128, 8, 8]), ALU.subtract, t1)
                t_es = act(es, es, ACT.Exp, t)
                pkf = pk.rearrange("p a b -> p (a b)")
                t1 = ts(ab[:, 0], pkf, 3, None, ALU.logical_shift_right, None, t1)
                t1 = ts(ab[:, 1], pkf, 7, None, ALU.bitwise_and, None, t1)
                t1 = cp(abf, ab, t1)
                io = iota8.unsqueeze(1).to_broadcast([128, 64, 8])
                eqh = eq.rearrange("p (h r) a -> p h r a", h=8)
                for q in range(2):
                    t1 = tt(eq, abf[:, q].unsqueeze(2).to_broadcast([128, 64, 8]), io, ALU.is_equal, t1)
                    t1 = tt(eqh, eqh, I8f[:, 8 * q:8 * q + 8, :].unsqueeze(2).to_broadcast([128, 8, 8, 8]), ALU.mult, t1)
                    t1 = red(ixy[:, q], eq, ALU.add, t1)
                t1 = ts(ge, ixy[:, 1], 32.0, None, ALU.is_ge, None, t1)

                def dup(v):
                    return v.unsqueeze(1).to_broadcast([128, 2, 64])
                t1 = stt(Z[:, 0], dup(ixy[:, 0]), 2.0, dup(ge), ALU.mult, ALU.add, t1)
                t1 = stt(Z[:, 1], dup(ge), -32.0, dup(ixy[:, 1]), ALU.mult, ALU.add, t1)
                t2 = red(ss, es, ALU.add, t_es)
                t2 = recip(ss, ss, t2)
                t2 = tt(es, es, ss.unsqueeze(2).to_broadcast([128, 8, 8]), ALU.mult, t2)
                t_Z = cp(Z[:, 2], dup(es.rearrange("p a b -> p (a b)")), t2)
                for i in range(3):
                    t = tr(bank(6)[:, 128 * i:128 * i + 128], Z[:, i].rearrange("p a b -> p (a b)"), t_Z, *free[6],
                           sig=(i == 2))
                tp = bank(6)[:, 0:384].rearrange("p (a b) -> p a b", a=3)
                t1 = cp(R3[0:64], tp[0:64, :, 0:64], t)
                t1 = cp(R3[64:128], tp[64:128, :, 64:128], t)
                free[6] = (t1,)
                for i in range(4):
                    t2 = ts(xh16[:, i], R3[:, 0], -32.0 * i, None, ALU.add, None, t1)
                t2 = cp(xl16, R3[:, 1], t1)
                t2 = cp(wv[:, 0], R3[:, 2], t1)
                t2 = tt(wv[:, 1], R3[:, 2], wv[:, 0], ALU.subtract, t2)
                tW_read = t_A.get("w")
                for i in range(4):
                    t3 = tt(X[:, 32 * i:32 * i + 32, :], iot, xh16[:, i].unsqueeze(1).to_broadcast([128, 32, 64]),
                            ALU.is_equal, t2, t_iot, tW_read)
                t3 = tt(Y, iot, xl16.unsqueeze(1).to_broadcast([128, 32, 64]), ALU.is_equal, t2)
                for i in range(2):
                    t3 = tt(Y12[:, i], Y, wv[:, i].unsqueeze(1).to_broadcast([128, 32, 64]), ALU.mult, t3)
                for r in range(4):
                    for gI in range(2):
                        b = 4 + gI
                        p0 = 64 * gI
                        for q in range(16):
                            tk = 16 * r + q
                            for i in range(2):
                                t = mm(bank(b)[:, 32 * q:32 * q + 32], X[p0:p0 + 64, :, tk], Y12[p0:p0 + 64, i, :, tk],
                                       i == 0, i == 1, t3, *free[b], sig=(q == 15 and i == 1))
                        g0 = 128 * bb + 64 * gI + 16 * r
                        gv = G[:, :, g0:g0 + 16]
                        t1 = tt(gv, gv, bank(b).rearrange("p (t j) -> p j t", j=32), ALU.mult, t, t_G)
                        free[b] = (t1,)
                t_A["w"] = t
                for j in range(32):
                    t = mm(bank(7)[:, 0:256], G[:, j, 128 * bb:128 * bb + 128], kout[:, j, :], j == 0, j == 31, t1,
                           t_kout, *free[7], sig=(j == 31))
                t_Gread = t
                t_x1 = tt(x1[:, bb], bank(7)[:, 0:256], xr[:, bb], ALU.add, t, t_xr, t_st[bb])
                t_xr_read[bb] = t_x1
                t_st[bb] = dma("sync", x1d[8 * blk:8 * blk + 8].rearrange("t b d -> (t b) d"), x1[:, bb], s_x1[bb], t_x1)
                for c in range(2):
                    t = tr(bank(7)[:, 256 + 128 * c:384 + 128 * c], x1[:, bb, 128 * c:128 * c + 128], t_x1, sig=(c == 1))
                t = act(x1T[:, :, n0:n0 + 128], bank(7)[:, 256:512].rearrange("p (a b) -> p a b", a=2), ACT.Copy, t)
                free[7] = (t_x1, t)
        t_x1s = list(t_st)
        barrier()
        if dbg:
            dma("sync", dbg["x1T"], x1T, s)

        arena.at = after_a
        hall = take(32, 256)
        hT = take(2, T + 1, NB)
        mark2 = arena.at
        Wx, Wh, bb_ = take(2, 1024), take(2, 1024), take(8)
        t_wx = [load(Wx, "Wx"), load(Wh, "Wh"), load(bb_, "lb")]
        t_h0 = load(hT[:, :, 0, :], "h0T")
        xW = [take(32, 8, 16) for _ in range(2)]
        cst = take(2, 16)
        gt = [take(8, 16) for _ in range(2)]
        m1, m2, th = take(2, 16), take(2, 16), take(2, 16)
        t_c = op("vector", lambda e: e.memset(cst, 0.0))
        free = [()] * 8
        xw_read = [None, None]
        t_h = t_h0
        xw_tok = {}

        def make_xw(s):
            for c in range(8):
                b = c % 2
                for k in range(2):
                    t = mm(bank(b), Wx[:, k, 128 * c:128 * c + 128], x1T[:, k, 512 * s:512 * s + 512], k == 0, k == 1,
                           *t_wx, *free[b], sig=(k == 1))
                t = act(xW[s % 2][:, :, c, :], bank(b).rearrange("p (t b) -> p t b", b=16), ACT.Identity, t,
                        xw_read[s % 2], bias=bb_[:, c:c + 1])
                free[b] = (t,)
            xw_tok[s] = t

        make_xw(0)
        for tstep in range(T):
            if tstep % 32 == 4 and tstep // 32 + 1 < 8:
                make_xw(tstep // 32 + 1)
            s = tstep // 32
            b = 2 + tstep % 2
            o = bank(b)[:, 0:128]
            t = mm(o, ident, xW[s % 2][:, tstep % 32].rearrange("p a b -> p (a b)"), True, False, xw_tok[s], t_id,
                   *free[b], sig=(tstep % 32 == 31))
            if tstep % 32 == 31:
                xw_read[s % 2] = t
            for c in (2, 3, 0, 1, 6, 7, 4, 5):
                for k in range(2):
                    t = mm(o[:, 16 * c:16 * c + 16], Wh[:, k, 128 * c:128 * c + 128], hT[:, k, tstep, :], False, c == 5 and k == 1,
                           t_h, sig=(k == 1))
            g = gt[tstep % 2]
            t_g = act(g[:, 0:6], o[:, 0:96].rearrange("p (a b) -> p a b", b=16), ACT.Sigmoid, t)
            t_g2 = act(g[:, 6:8], o[:, 96:128].rearrange("p (a b) -> p a b", b=16), ACT.Tanh, t)
            free[b] = (t_g2,)
            t1 = tt(m1, g[:, 2:4], cst, ALU.mult, t_g, t_c)
            t2 = tt(m2, g[:, 0:2], g[:, 6:8], ALU.mult, t_g2)
            t_c = tt(cst, m1, m2, ALU.add, t1, t2)
            t3 = act(th, cst, ACT.Tanh, t_c)
            t_h = tt(hT[:, :, tstep + 1, :], g[:, 4:6], th, ALU.mult, t3)
        barrier()
        if dbg:
            dma("sync", dbg["hT"], hT[:, :, 1:T + 1, :], s if False else P.new_sem("dbg1"))

        arena.at = mark2
        lnp = take(4, 2)
        wqkv, wo = take(2, 768), take(2, 256)
        bqk, msk = take(4), take(2)
        bv, bo = take(256), take(256)
        t_l = [load(lnp, "ln"), load(wqkv, "wqkv"), load(wo, "wo"), load(bqk, "bqk"), load(msk, "mask"), load(bv, "bv"),
               load(bo, "bo")]
        stt6, mv1, rstd = take(32, 6), take(32, 2), take(32)
        bm = take(2, 2)
        free = [()] * 8
        for m in range(32):
            q, thf = m // 2, m % 2
            b = m % 2
            for c in range(2):
                t = tr(bank(b)[:, 128 * c:128 * c + 128], hT[:, c, 1 + 128 * thf:129 + 128 * thf, q], *free[b],
                       sig=(c == 1))
            t = act(hall[:, m], bank(b)[:, 0:256], ACT.Copy, t)
            free[b] = (t,)
            t = op("vector", lambda e, m=m: e.bn_stats(stt6[:, m], hall[:, m]), t)
            t = op("vector", lambda e, m=m: e.bn_aggr(mv1[:, m], stt6[:, m]), t)
        t = act(rstd, mv1[:, :, 1], ACT.Sqrt, t, t_eps, bias=epst)
        t_rstd = recip(rstd, rstd, t)
        for c in range(2):
            t_bm = tt(bm[:, c, :], bqk[:, 2 + c:3 + c].to_broadcast([128, 2]), msk, ALU.mult, *t_l)
        barrier()
        arena_m = arena.at
        xh = take(2, 256)
        h1T, qT, kE = take(2, 256), take(2, 256), take(2, 2, 256)
        vv = take(2, 256)
        Pp = [take(2, 256) for _ in range(3)]
        PT = [take(4, 128) for _ in range(3)]
        nm = [take(2) for _ in range(4)]
        sm = take(2, 16)
        rs = take(2, 16)
        on, oT = take(2, 256), take(2, 256)
        free = [()] * 8
        t_fin = None
        t_sm_read = None
        for sq in range(16):
            for j in range(2):
                m = 2 * sq + j
                t = ts(xh[:, j], hall[:, m], mv1[:, m, 0:1], rstd[:, m:m + 1], ALU.subtract, ALU.mult, t_rstd)
            for c in range(2):
                for j in range(2):
                    t1 = tr(bank(c)[:, 128 * j:128 * j + 128], xh[:, j, 128 * c:128 * c + 128], t, *free[c],
                            sig=(j == 1))
                t_n = act(h1T[:, c], bank(c)[:, 0:256], ACT.Identity, t1, *t_l, bias=lnp[:, 1, c:c + 1],
                          scale=lnp[:, 0, c:c + 1])
                free[c] = (t_n,)
            for c in range(4):
                b = c % 2
                for k in range(2):
                    t = mm(bank(b)[:, 0:256], wqkv[:, k, 128 * c:128 * c + 128], h1T[:, k], k == 0, k == 1, t_n,
                           *free[b], sig=(k == 1))
                if c < 2:
                    t_q = ts(qT[:, c], bank(b)[:, 0:256], bqk[:, c:c + 1], 0.25, ALU.add, ALU.mult, t)
                    free[b] = (t_q,)
                else:
                    for eo in range(2):
                        t_k2 = act(kE[:, c - 2, eo], bank(b)[:, 0:256], ACT.Identity, t, t_bm,
                                   bias=bm[:, c - 2, eo:eo + 1], scale=msk[:, eo:eo + 1])
                    free[b] = (t_k2,)
            for j in range(2):
                for k in range(2):
                    t = mm(bank(j)[:, 0:256], h1T[:, k, 128 * j:128 * j + 128], wqkv[:, k, 512:768], k == 0, k == 1,
                           *free[j], sig=(k == 1))
                t_v = tt(vv[:, j], bank(j)[:, 0:256], bv, ALU.add, t)
                free[j] = (t_v,)
            pend = []

            def values(qb, pr_, b, P_, t_e):
                for hh in range(2):
                    for kb in range(2):
                        t = tr(bank(b)[:, 128 * (2 * hh + kb):128 * (2 * hh + kb) + 128],
                               P_[:, hh, 128 * kb:128 * kb + 128], t_e, *free[b], sig=(hh == 1 and kb == 1))
                pt = PT[cnt[0] % 3]
                t = cp(pt, bank(b).rearrange("p (a b) -> p a b", a=4), t, *ptr_[cnt[0] % 3])
                free[b] = (t,)
                ob = bank(6 + qb)
                for hh in range(2):
                    h = 2 * pr_ + hh
                    for kb in range(2):
                        t2 = mm(ob[:, 16 * h:16 * h + 16], pt[:, 2 * hh + kb, :], vv[:, kb, 16 * h:16 * h + 16],
                                kb == 0, kb == 1, t, t_v, *free[6 + qb], sig=(hh == 1 and kb == 1))
                ptr_[cnt[0] % 3] = (t2,)
                cnt[0] += 1
                return t2

            cnt = [0]
            ptr_ = [(), (), ()]
            ppr = [(), (), ()]
            t_o = [None, None]
            n = 0
            for qb in range(2):
                for pr_ in range(8):
                    c, p0 = pr_ // 4, 32 * (pr_ % 4)
                    b = 2 + n % 2
                    for hh in range(2):
                        t = mm(bank(b)[:, 256 * hh:256 * hh + 256], qT[p0:p0 + 32, c, 128 * qb:128 * qb + 128],
                               kE[p0:p0 + 32, c, hh, :], True, True, t_q, t_k2, *free[b], sig=(hh == 1))
                    nm_ = nm[n % 4]
                    t1 = red(nm_, bank(b).rearrange("p (a b) -> p a b", a=2), ALU.max, t, neg=True)
                    P_ = Pp[n % 3]
                    for hh in range(2):
                        t2 = act(P_[:, hh], bank(b)[:, 256 * hh:256 * hh + 256], ACT.Exp, t1, *ppr[n % 3], t_sm_read,
                                 bias=nm_[:, hh:hh + 1], acc=sm[:, qb, 2 * pr_ + hh:2 * pr_ + hh + 1])
                    free[b] = (t2,)
                    pend.append((qb, pr_, 4 + n % 2, P_, t2, n % 3))
                    n += 1
                    if len(pend) == 2:
                        a = pend.pop(0)
                        t = values(*a[:5])
                        t_o[a[0]] = t
                        ppr[a[5]] = (t,)
            a = pend.pop(0)
            t_o[1] = values(*a[:5])
            t = recip(rs, sm, t2)
            t_sm_read = t
            for qb in range(2):
                t_on = tt(on[:, qb].rearrange("p (a b) -> p a b", a=16),
                          bank(6 + qb)[:, 0:256].rearrange("p (a b) -> p a b", a=16),
                          rs[:, qb].unsqueeze(2).to_broadcast([128, 16, 16]), ALU.mult, t, t_o[qb])
                free[6 + qb] = (t_on,)
            for c in range(2):
                for j in range(2):
                    t1 = tr(bank(c)[:, 128 * j:128 * j + 128], on[:, j, 128 * c:128 * c + 128], t_on, *free[c],
                            sig=(j == 1))
                t_oT = act(oT[:, c], bank(c)[:, 0:256], ACT.Copy, t1)
                free[c] = (t_oT,)
            for j in range(2):
                m = 2 * sq + j
                for k in range(2):
                    t = mm(bank(j)[:, 0:256], oT[:, k, 128 * j:128 * j + 128], wo[:, k], k == 0, k == 1, t_oT,
                           *free[j], sig=(k == 1))
                t = tt(hall[:, m], bank(j)[:, 0:256], hall[:, m], ALU.add, t)
                free[j] = (t,)
                t = tt(hall[:, m], hall[:, m], bo, ALU.add, t)
                t = op("vector", lambda e, m=m: e.bn_stats(stt6[:, m], hall[:, m]), t)
                t_s2 = op("vector", lambda e, m=m: e.bn_aggr(mv1[:, m], stt6[:, m]), t)
        barrier()
        if dbg:
            dma("sync", dbg["x2"], hall, P.new_sem("dbg2"))

        arena.at = base
        h2T = take(2, N)
        assert arena.at <= after_a
        arena.at = arena_m
        gw, gb_ = take(2, 8), take(8)
        b1, b2 = take(8, 8), take(256)
        t_g = [load(gw, "gate_w"), load(gb_, "gate_b"), load(b1, "b1"), load(b2[0:8], "b2")]
        W1 = [take(2, 1024) for _ in range(2)]
        W2 = [take(8, 256) for _ in range(2)]
        s_w = [P.new_sem(f"ew{i}") for i in range(2)]
        t_ew = {}

        def load_e(e, *after):
            dma("sync", W1[e % 2], I["W1"][:, e], s_w[e % 2], *after)
            t_ew[e] = dma("sync", W2[e % 2], I["W2"][:, e], s_w[e % 2])

        load_e(0)
        load_e(1)
        xh = [take(256) for _ in range(2)]
        lgt, mm8, ii8, ii8f = take(32, 8), take(32, 8), take(32, 8, dt=u32), take(32, 8)
        o1, o2, ew = take(32, 8), take(32, 8), take(32, 8)
        dd, g1, g2 = take(32), take(32), take(32)
        ewT = take(2, 128)
        hid = [take(8, 512) for _ in range(2)]
        free = [()] * 8
        t = act(rstd, mv1[:, :, 1], ACT.Sqrt, bias=epst)
        t_rstd = recip(rstd, rstd, t)
        t_xr2 = [None, None]
        for m in range(32):
            x_ = xh[m % 2]
            t = ts(x_, hall[:, m], mv1[:, m, 0:1], rstd[:, m:m + 1], ALU.subtract, ALU.mult, t_rstd, t_xr2[m % 2])
            b = m % 2
            for c in range(2):
                t1 = tr(bank(b)[:, 128 * c:128 * c + 128], x_[:, 128 * c:128 * c + 128], t, *free[b], sig=(c == 1))
            t_xr2[m % 2] = t1
            for c in range(2):
                t2 = act(h2T[:, c, 128 * m:128 * m + 128], bank(b)[:, 128 * c:128 * c + 128], ACT.Identity, t1,
                         bias=lnp[:, 3, c:c + 1], scale=lnp[:, 2, c:c + 1])
            free[b] = (t2,)
            for k in range(2):
                t = mm(bank(2)[:, 8 * m:8 * m + 8], h2T[:, k, 128 * m:128 * m + 128], gw[:, k], k == 0, k == 1, t2,
                       *t_g, sig=(k == 1))
        t = tt(lgt, bank(2)[:, 0:256].rearrange("p (a b) -> p a b", b=8), gb_.unsqueeze(1).to_broadcast([128, 32, 8]),
               ALU.add, t)
        for m in range(32):
            t1 = mx8(mm8[:, m], lgt[:, m], t)
        for m in range(32):
            t2 = ix8(ii8[:, m], mm8[:, m], lgt[:, m], t1)
        t = cp(ii8f, ii8, t2)
        t1 = tt(dd, mm8[:, :, 1], mm8[:, :, 0], ALU.subtract, t)
        t1 = act(g2, dd, ACT.Exp, t1)
        t1 = ts(g1, g2, 1.0, None, ALU.add, None, t1)
        t1 = recip(g1, g1, t1)
        t1 = tt(g2, g2, g1, ALU.mult, t1)
        io = iota8.unsqueeze(1).to_broadcast([128, 32, 8])
        t2 = tt(o1, ii8f[:, :, 0:1].to_broadcast([128, 32, 8]), io, ALU.is_equal, t)
        t2 = tt(o2, ii8f[:, :, 1:2].to_broadcast([128, 32, 8]), io, ALU.is_equal, t)
        t2 = tt(o1, o1, g1.unsqueeze(2).to_broadcast([128, 32, 8]), ALU.mult, t1, t2)
        t2 = tt(o2, o2, g2.unsqueeze(2).to_broadcast([128, 32, 8]), ALU.mult, t2)
        t_ewt = tt(ew, o1, o2, ALU.add, t2)
        t_er = [None, None]
        for m in range(32):
            b = m % 2
            t = tr(bank(b)[0:8, 0:128], ew[:, m], t_ewt, *free[b], sig=True)
            t = act(ewT[0:8, b], bank(b)[0:8, 0:128], ACT.Copy, t, t_er[b])
            free[b] = (t,)
            t = mm(bank(3 + b)[:, 0:256], ewT[0:8, b], b2[0:8], True, True, t, *free[3 + b], sig=True)
            t_er[b] = t
            t_y = tt(hall[:, m], bank(3 + b)[:, 0:256], hall[:, m], ALU.add, t)
            free[3 + b] = (t_y,)
        barrier()
        free = [()] * 8
        hid_read = [(), ()]
        n = 0
        for e in range(8):
            for s in range(8):
                h_ = hid[s % 2]
                for f in range(8):
                    b = n % 4
                    n += 1
                    for k in range(2):
                        t = mm(bank(b), W1[e % 2][:, k, 128 * f:128 * f + 128], h2T[:, k, 512 * s:512 * s + 512], k == 0,
                               k == 1, t_ew[e], *free[b], sig=(k == 1))
                    if f % 4 != 3:
                        t_r1 = act(h_[:, f], bank(b), ACT.Relu, t, *hid_read[s % 2], bias=b1[:, e, f:f + 1])
                        free[b] = (t_r1,)
                    else:
                        t_r2 = ts(h_[:, f], bank(b), b1[:, e, f:f + 1], 0.0, ALU.add, ALU.max, t, *hid_read[s % 2])
                        free[b] = (t_r2,)
                for j in range(4):
                    m = 4 * s + j
                    b = 4 + j
                    for f in range(8):
                        t = mm(bank(b)[:, 0:256], h_[:, f, 128 * j:128 * j + 128], W2[e % 2][:, f], f == 0, f == 7, t_r1,
                               t_r2, *free[b], sig=(f == 7))
                    t_y = stt(hall[:, m], bank(b)[:, 0:256], ew[:, m, e:e + 1], hall[:, m], ALU.mult, ALU.add, t)
                    free[b] = (t_y,)
                hid_read[s % 2] = (t,)
            if e + 2 < 8:
                load_e(e + 2, t)
        xi = [take(256) for _ in range(4)]
        s_i = [P.new_sem(f"xi{i}") for i in range(4)]
        s_o = [P.new_sem(f"xo{i}") for i in range(4)]
        t_o = [None] * 4
        for m in range(32):
            q, thf = m // 2, m % 2
            i = m % 4
            t = dma("sync", xi[i], x1d[128 * thf:128 * thf + 128, q, :], s_i[i], t_o[i], *t_x1s)
            t = tt(xi[i], xi[i], hall[:, m], ALU.add, t, t_y)
            t_o[i] = dma("sync", out[q, 128 * thf:128 * thf + 128, :], xi[i], s_o[i], t)
        P.wait("sync", t_o)
        block = ctx.enter_context(nc.Block())
        P.emit(block)


def layout(i):
    import numpy as np

    def kp(a, k):
        return np.ascontiguousarray(a.reshape(k, 128, *a.shape[1:]).swapaxes(0, 1))

    def rep(a):
        return np.ascontiguousarray(np.broadcast_to(a.reshape(1, -1), (128, a.size)))

    x = i["x"]
    cond = i["cond_1024"]
    cT = kp(np.ascontiguousarray(cond.T), 2)
    d = {
        "xT": kp(np.ascontiguousarray(x.transpose(2, 1, 0)).reshape(256, N), 2),
        "xtb": np.ascontiguousarray(x.transpose(1, 0, 2)).reshape(32, 128, 256),
        "condT": np.ascontiguousarray(np.tile(cT, (1, 1, 8))),
        "h0T": cT,
        "rW": kp(i["L0_cond_router_W"], 4),
        "rb": rep(i["L0_cond_router_bias"]),
        "w1": kp(i["L0_cond_w1"], 2), "w3": kp(i["L0_cond_w3"], 2), "w2": kp(i["L0_cond_w2"], 4),
        "W1e": np.ascontiguousarray(i["L0_cond_W1e"].reshape(8, 2, 128, 256).transpose(2, 0, 1, 3)),
        "W2e": np.ascontiguousarray(i["L0_cond_W2e"].reshape(8, 2, 128, 256).transpose(2, 0, 1, 3)),
        "gamma": np.ascontiguousarray(i["L0_ffn_gamma"].reshape(2, 128).T),
        "beta": np.ascontiguousarray(i["L0_ffn_beta"].reshape(2, 128).T),
        "wq": kp(i["L0_ffn_w_q"], 16),
        "keysT": np.ascontiguousarray(i["L0_ffn_keys"].transpose(3, 2, 0, 1).reshape(128, 16, 64)),
        "kinT": np.ascontiguousarray(i["L0_ffn_key_in"].reshape(128, 32, 2, 128).transpose(3, 2, 1, 0)),
        "kout": i["L0_ffn_key_out"].reshape(128, 32, 256),
        "Wx": kp(i["L1_cond_Wx"], 2), "Wh": kp(i["L1_cond_Wh"], 2),
        "lb": np.ascontiguousarray(i["L1_cond_b"].reshape(8, 128).T),
        "ln": np.ascontiguousarray(np.stack([i["L1_ffn_ln1_g"], i["L1_ffn_ln1_b"], i["L1_ffn_ln2_g"], i["L1_ffn_ln2_b"]])
                                   .reshape(4, 2, 128).transpose(2, 0, 1)),
        "wqkv": kp(i["L1_ffn_w_qkv"], 2),
        "bqk": np.ascontiguousarray(i["L1_ffn_b_qkv"][:512].reshape(4, 128).T),
        "bv": rep(i["L1_ffn_b_qkv"][512:]),
        "wo": kp(i["L1_ffn_w_o"], 2), "bo": rep(i["L1_ffn_b_o"]),
        "gate_w": kp(i["L1_ffn_gate_w"], 2), "gate_b": rep(i["L1_ffn_gate_b"]),
        "W1": np.ascontiguousarray(i["L1_ffn_W1"].reshape(8, 2, 128, 1024).transpose(2, 0, 1, 3)),
        "b1": np.ascontiguousarray(i["L1_ffn_b1"].reshape(8, 8, 128).transpose(2, 0, 1)),
        "W2": np.ascontiguousarray(i["L1_ffn_W2"].reshape(8, 8, 128, 256).transpose(2, 0, 1, 3)),
        "b2": i["L1_ffn_b2"],
        "ident": np.eye(128, dtype=np.float32),
        "iota8": np.tile(np.arange(8, dtype=np.float32), (128, 1)),
        "iota32": np.ascontiguousarray(np.broadcast_to(np.arange(32, dtype=np.float16)[None, :, None], (128, 32, 64))),
        "mask": np.stack([(np.arange(128) // 16 % 2 == 0), (np.arange(128) // 16 % 2 == 1)], 1).astype(np.float32),
    }
    return d


def kernel(**inputs):
    import numpy as np
    import concourse.bacc as bacc
    from concourse.bass_utils import run_bass_kernel_spmd

    nc = bacc.Bacc("TRN2", target_bir_lowering=False, num_devices=1)
    arrays, ins = {}, {}
    for name, a in layout({k: np.asarray(v) for k, v in inputs.items()}).items():
        a = np.ascontiguousarray(a)
        arrays[f"in_{name}"] = a
        ins[name] = nc.dram_tensor(f"in_{name}", a.shape, mybir.dt.from_np(a.dtype), kind="ExternalInput").ap()
    out = nc.dram_tensor("out_0", (NB, T, D), mybir.dt.float32, kind="ExternalOutput").ap()
    build(nc, ins, out)
    r = run_bass_kernel_spmd(nc, [arrays], core_ids=[0])
    return r.results[0]["out_0"]
```

```python
import concourse.bass as bass
from concourse import mybir
from contextlib import ExitStack

NB, T, D = 16, 256, 256
N = NB * T


class Program:

    def __init__(self, nc, ctx):
        self.nc, self.ctx = nc, ctx
        self.q = {k: [] for k in ("tensor", "vector", "scalar", "gpsimd", "sync")}
        self.sem = {k: ctx.enter_context(nc.semaphore("s_" + k)) for k in self.q}
        self.count = {k: 0 for k in self.q}
        self.seen = {k: {} for k in self.q}
        self.nsem = 0
        self.dma_count = {}
        self.dsems = []

    def wait(self, eng, after):
        for tok in after:
            if tok is None:
                continue
            sem, v = tok
            if self.seen[eng].get(id(sem), 0) < v:
                self.seen[eng][id(sem)] = v
                self.q[eng].append(lambda e, sem=sem, v=v: e.wait_ge(sem, v))

    def op(self, eng, f, *after, sig=True):
        self.wait(eng, after)
        if not sig:
            self.q[eng].append(f)
            return None
        self.count[eng] += 1
        s = self.sem[eng]
        self.q[eng].append(lambda e: f(e).then_inc(s, 1))
        return (s, self.count[eng])

    def new_sem(self, name):
        s = self.ctx.enter_context(self.nc.semaphore(name))
        self.dma_count[id(s)] = 0
        self.dsems.append(s)
        return s

    def dma(self, eng, out, in_, sem, *after):
        self.wait(eng, after)
        self.dma_count[id(sem)] += 16
        self.q[eng].append(lambda e: e.dma_start(out, in_).then_inc(sem, 16))
        return (sem, self.dma_count[id(sem)])

    def emit(self, block):
        for name in self.q:
            def body(e, items=self.q[name]):
                for f in items:
                    f(e)
            start = {"tensor": block.tensor, "vector": block.vector, "scalar": block.scalar,
                            "gpsimd": block.gpsimd, "sync": block.sync}[name]
            start(body)


class Arena:
    def __init__(self, t, words):
        self.t, self.words, self.at = t, words, 0

    def take(self, *dims, dt=None):
        n = 1
        for d in dims:
            n *= d
        half = dt is not None and mybir.dt.size(dt) == 2
        w = (n + 1) // 2 if half else n
        w = (w + 7) // 8 * 8
        v = self.t[:, self.at:self.at + w]
        self.at += w
        assert self.at <= self.words, (self.at, self.words)
        if dt is not None:
            v = v.bitcast(dt)
        v = v[:, 0:n]
        if len(dims) == 2:
            v = v.rearrange("p (a b) -> p a b", a=dims[0])
        elif len(dims) == 3:
            v = v.rearrange("p (a b c) -> p a b c", a=dims[0], b=dims[1])
        elif len(dims) == 4:
            v = v.rearrange("p (a b c d) -> p a b c d", a=dims[0], b=dims[1], c=dims[2])
        return v


def build(nc, I, out, dbg=None):
    f32, f16, u32 = mybir.dt.float32, mybir.dt.float16, mybir.dt.uint32
    ALU, ACT, AX = mybir.AluOpType, mybir.ActivationFunctionType, mybir.AxisListType
    WORDS = 52000
    ctx = ExitStack()
    with ctx:
        P = Program(nc, ctx)
        arena = Arena(ctx.enter_context(nc.sbuf_tensor("arena", [128, WORDS], f32)), WORDS)
        ps = ctx.enter_context(nc.psum_tensor("ps", [128, 4096], f32))
        x1d = nc.dram_tensor("x1_scratch", [T, NB, D], f32, kind="Internal").ap()
        op, dma = P.op, P.dma
        take = arena.take

        def bank(b, n=1):
            return ps[:, 512 * b:512 * (b + n)]

        free = [()] * 8

        def mm(o, l, r, start, stop, *after, sig=False):
            return op("tensor", lambda e: e.matmul(o, l, r, start=start, stop=stop), *after, sig=sig)

        def tr(o, i, *after, sig=False):
            return op("tensor", lambda e: e.transpose(o, i, ident), *after, sig=sig)

        def act(o, i, fn, *after, bias=0.0, scale=1.0, acc=None):
            if acc is None:
                return op("scalar", lambda e: e.activation(o, i, fn, bias=bias, scale=scale), *after)
            return op("scalar", lambda e: e.activation(o, i, fn, bias=bias, scale=scale, accum_out=acc), *after)

        def tt(o, a, b, alu, *after):
            return op("vector", lambda e: e.tensor_tensor(o, a, b, alu), *after)

        def ts(o, a, s1, s2, o0, o1, *after):
            if o1 is None:
                return op("vector", lambda e: e.tensor_scalar(o, a, s1, None, o0), *after)
            return op("vector", lambda e: e.tensor_scalar(o, a, s1, s2, o0, o1), *after)

        def stt(o, a, s, b, o0, o1, *after):
            return op("vector", lambda e: e.scalar_tensor_tensor(o, a, s, b, o0, o1), *after)

        def cp(o, i, *after):
            return op("vector", lambda e: e.tensor_copy(o, i), *after)

        def red(o, i, alu, *after, neg=False):
            return op("vector", lambda e: e.tensor_reduce(o, i, AX.X, alu, negate=neg), *after)

        def mx8(o, i, *after):
            return op("vector", lambda e: e.max(o, i), *after)

        def ix8(o, m, v, *after):
            return op("vector", lambda e: e.max_index(o, m, v), *after)

        def recip(o, i, *after):
            return op("vector", lambda e: e.reciprocal(o, i), *after)

        def load(tile, name, *after, eng="sync"):
            s = P.new_sem("l_" + name)
            return dma(eng, tile, I[name], s, *after)

        def barrier():
            toks = [(P.sem[k], P.count[k]) for k in P.q if P.count[k]]
            for k in P.q:
                P.wait(k, toks)

        ident = take(128)
        t_id = load(ident, "ident")
        iota8 = take(8)
        t_i8 = load(iota8, "iota8")
        epst = take(1)
        t_eps = op("vector", lambda e: e.memset(epst, 1e-5))
        base = arena.at

        def finish():
            P.wait("sync", [(v, P.dma_count[id(v)]) for v in P.dsems])
            P.emit(ctx.enter_context(nc.Block()))

        xcT = take(2, N)
        after_a = arena.at
        xT = [take(2, 512) for _ in range(2)]
        s_xT = [P.new_sem(f"xT{i}") for i in range(2)]
        cT, rW, rb = take(2, 128), take(4, 8), take(8)
        t_r = [load(cT, "condT"), load(rW, "rW"), load(rb, "rb")]
        w1, w3, w2 = take(2, 512), take(2, 512), take(4, 256)
        t_xT = {}

        def load_x(s, *after):
            t_xT[s] = dma("sync", xT[s % 2], I["xT"][:, :, 512 * s:512 * (s + 1)], s_xT[s % 2], *after)

        load_x(0)
        t_w = [load(w1, "w1"), load(w3, "w3"), load(w2, "w2")]
        W1e, W2e = take(8, 2, 256), take(8, 2, 256)
        t_e = [load(W1e, "W1e"), load(W2e, "W2e")]
        load_x(1)
        TL = take(8)
        comb = take(4, 8)
        sg, sl, m8, oh = take(4, 8), take(4, 8), take(4, 8), take(2, 4, 8)
        i8 = take(4, 8, dt=u32)
        i8f, sel, dn, fl, rr = take(4, 8), take(2, 4, 8), take(4), take(4), take(4)
        sv = take(2, 4)
        silu_s, hs = take(512), take(4, 512)
        he = [take(2, 512) for _ in range(2)]
        acc = take(4, 256)
        st = take(2, 8, 6)

        for k in range(2):
            t = mm(bank(0)[:, 0:8], cT[:, k, :], rW[:, 2 + k, :], k == 0, k == 1, *t_r, sig=(k == 1))
        t_TL = cp(TL, bank(0)[:, 0:8], t)
        free[0] = (t_TL,)
        t_acc_read = None
        t_he = [(), ()]
        t_hs_read = None
        t_bn = None
        for s in range(8):
            x_ = xT[s % 2]
            for j in range(4):
                for k in range(2):
                    t = mm(bank(0)[:, 8 * j:8 * j + 8], x_[:, k, 128 * j:128 * j + 128], rW[:, k, :], k == 0, k == 1,
                           t_xT[s], *free[0], sig=(j == 3 and k == 1))
            lg = bank(0)[:, 0:32].rearrange("p (a b) -> p a b", a=4)
            t = tt(sl, lg, TL.unsqueeze(1).to_broadcast([128, 4, 8]), ALU.add, t, t_TL)
            free[0] = (t,)
            t_s = act(sg, sl, ACT.Sigmoid, t)
            t = tt(sl, sg, rb.unsqueeze(1).to_broadcast([128, 4, 8]), ALU.add, t_s)
            for j in range(4):
                t1 = mx8(m8[:, j, :], sl[:, j, :], t)
            for j in range(4):
                t1 = ix8(i8[:, j, :], m8[:, j, :], sl[:, j, :], t1)
            t = cp(i8f, i8, t1)
            io = iota8.unsqueeze(1).to_broadcast([128, 4, 8])
            for k in range(2):
                t1 = tt(oh[:, k], i8f[:, :, k:k + 1].to_broadcast([128, 4, 8]), io, ALU.is_equal, t, t_i8)
                t1 = tt(sel[:, k], oh[:, k], sg, ALU.mult, t1)
                t1 = red(sv[:, k], sel[:, k], ALU.add, t1)
            t = tt(dn, sv[:, 0], sv[:, 1], ALU.add, t1)
            t = ts(fl, dn, 1e-9, None, ALU.is_gt, None, t)
            t = ts(rr, dn, 1e-9, None, ALU.add, None, t)
            t = recip(rr, rr, t)
            t = tt(rr, rr, fl, ALU.mult, t)
            t = ts(fl, fl, -0.5, 0.5, ALU.mult, ALU.add, t)
            rrb = rr.unsqueeze(2).to_broadcast([128, 4, 8])
            flb = fl.unsqueeze(2).to_broadcast([128, 4, 8])
            t = tt(sel[:, 0], sel[:, 0], sel[:, 1], ALU.add, t)
            t = tt(sel[:, 0], sel[:, 0], rrb, ALU.mult, t)
            t = tt(oh[:, 0], oh[:, 0], oh[:, 1], ALU.add, t)
            t = tt(oh[:, 0], oh[:, 0], flb, ALU.mult, t)
            t_comb = tt(comb, oh[:, 0], sel[:, 0], ALU.add, t)
            for c in range(4):
                for w, b in ((w1, 2), (w3, 3)):
                    for k in range(2):
                        t = mm(bank(b), w[:, k, 128 * c:128 * c + 128], x_[:, k, :], k == 0, k == 1, t_xT[s],
                               *t_w, *free[b], sig=(k == 1))
                    if b == 2:
                        t_u = t
                t_si = act(silu_s, bank(2), ACT.Silu, t_u, t_hs_read)
                t_hs = tt(hs[:, c, :], silu_s, bank(3), ALU.mult, t_si, t)
                t_hs_read = t_hs
                free[2], free[3] = (t_si,), (t_hs,)
            for j in range(4):
                for c in range(4):
                    t = mm(bank(4 + j // 2)[:, 256 * (j % 2):256 * (j % 2) + 256], hs[:, c, 128 * j:128 * j + 128],
                           w2[:, c, :], c == 0, c == 3, t_hs, *free[4 + j // 2], sig=(c == 3))
                if j % 2:
                    b = 4 + j // 2
                    t_acc = act(acc[:, j - 1:j + 1, :], bank(b).rearrange("p (a b) -> p a b", a=2), ACT.Copy, t,
                                t_acc_read)
                    free[b] = (t_acc,)
            for e in range(8):
                h_ = he[e % 2]
                for c in range(2):
                    b = 2 + c
                    for k in range(2):
                        t = mm(bank(b), W1e[:, e, k, 128 * c:128 * c + 128], x_[:, k, :], k == 0, k == 1, t_e[0],
                               *free[b], sig=(k == 1))
                    t_h = act(h_[:, c, :], bank(b), ACT.Gelu, t, *t_he[e % 2])
                    free[b] = (t_h,)
                for j in range(4):
                    b = 4 + j
                    o = bank(b)[:, 0:256]
                    for c in range(2):
                        t = mm(o, h_[:, c, 128 * j:128 * j + 128], W2e[:, e, c, :], c == 0, c == 1, t_h, t_e[1],
                               *free[b], sig=(c == 1))
                    t_a = stt(acc[:, j, :], o, comb[:, j, e:e + 1], acc[:, j, :], ALU.mult, ALU.add, t, t_acc, t_comb)
                    free[b] = (t_a,)
                t_acc = t_a
                t_he[e % 2] = (t,)
            if s + 2 < 8:
                load_x(s + 2, t_he[0][0], t_he[1][0])
            for c in range(2):
                b = c
                for j in range(4):
                    t = tr(bank(b)[:, 128 * j:128 * j + 128], acc[:, j, 128 * c:128 * c + 128], t_acc, t_id, *free[b],
                           sig=(j == 3))
                o = xcT[:, c, 512 * s:512 * s + 512]
                t_x = act(o, bank(b), ACT.Copy, t, scale=1.0 / 3.0)
                free[b] = (t_x,)
                t_bn = op("vector", lambda e, c=c, s=s, o=o: e.bn_stats(st[:, c, s, :], o), t_x)
            t_acc_read = t
        mv0 = take(2, 2)
        for c in range(2):
            t = op("vector", lambda e, c=c: e.bn_aggr(mv0[:, c, :], st[:, c].rearrange("p a b -> p (a b)")), t_bn)
        barrier()
        arena.at = after_a
        ga = take(2)
        ba = take(2)
        gb = [load(ga, "gamma"), load(ba, "beta")]
        mv = take(2, 2)
        t = cp(mv, mv0, t)
        a_, b_ = take(2), take(2)
        t = act(a_, mv[:, :, 1], ACT.Sqrt, t, t_eps, bias=epst)
        t = recip(a_, a_, t)
        t = tt(a_, a_, ga, ALU.mult, t, *gb)
        t = tt(b_, mv[:, :, 0], a_, ALU.mult, t)
        t_ab = tt(b_, ba, b_, ALU.subtract, t)
        if dbg:
            s = P.new_sem("dbg0")
            dma("sync", dbg["xcT"], xcT, s)

        if dbg and dbg.get('upto') == 1:
            return finish()
        bf16 = mybir.dt.bfloat16
        Kc = take(2, 1024)
        Wx = take(2, 1024)
        W3 = take(3, 2, 1024, dt=bf16)
        lb = take(8)
        h0 = take(2, 16)
        mark = arena.at
        wq, kT, Wh = take(16, 256), take(16, 64), take(2, 1024)
        wr_ = take(2, 1024)
        t_k = [load(wq, "wq"), load(kT, "keysT")]
        t_wx = [load(Wx, "Wx"), load(Wh, "Wh"), load(lb, "lb"), load(h0, "h0T")]
        for c in range(2):
            for g in range(16):
                b = 2 * c + g // 8
                t = mm(bank(b)[:, 64 * (g % 8):64 * (g % 8) + 64], wq[:, g, 128 * c:128 * c + 128], kT[:, g, :],
                       True, True, *t_k, sig=(g % 8 == 7))
                if g % 8 == 7:
                    t_Kc = cp(Kc[:, c, 512 * (g // 8):512 * (g // 8) + 512], bank(b), t)
        t = ts(Wx[:, :, 768:1024], Wx[:, :, 768:1024], 2.0, None, ALU.mult, None, *t_wx)
        t = ts(lb[:, 6:8], lb[:, 6:8], 2.0, None, ALU.mult, None, t)
        t = ts(Wh[:, :, 0:768], Wh[:, :, 0:768], 0.5, None, ALU.mult, None, t)
        t = cp(W3[:, 0], Wh, t)
        t = tt(wr_, Wh, W3[:, 0], ALU.subtract, t)
        t = cp(W3[:, 1], wr_, t)
        t_W3 = tt(W3[:, 2], wr_, W3[:, 1], ALU.subtract, t)
        t_h0 = ts(h0, h0, 2.0, None, ALU.mult, None, t)
        barrier()
        arena.at = mark
        kin, kout = take(2, 32, 128), take(32, 256)
        t_kin, t_kout = load(kin, "kinT"), load(kout, "kout")
        iot = take(32, 64, dt=f16)
        t_iot = load(iot, "iota32")
        G = take(32, 128)
        X = take(128, 64, dt=f16)
        Y12 = take(2, 32, 64, dt=f16)
        xn = take(2, 128)
        S8, I8, I8f = take(16, 8), take(16, 8, dt=u32), take(16, 8)
        pr = take(8, 8, 8)
        sc, pk = take(8, 8), take(8, 8, dt=u32)
        ab, abf = take(2, 64, dt=u32), take(2, 64)
        eq = take(64, 8)
        ixy = take(2, 64)
        ge, es, ss = take(64), take(8, 8), take(8)
        Z = take(3, 2, 64)
        R3 = take(3, 64)
        xh16 = take(4, 64, dt=f16)
        xl16, wv = take(64, dt=f16), take(2, 64, dt=f16)
        xr = take(2, 256)
        x1 = take(2, 256)
        xW = take(2, 8, 8, 16)
        cst, gt, pre = take(2, 16), take(2, 8, 16), take(8, 16)
        m1, m2, th, hr = take(2, 16), take(2, 16), take(2, 16), take(2, 16)
        h3 = take(2, 2, 3, 16, dt=bf16)
        s_xr = [P.new_sem(f"xr{i}") for i in range(2)]
        s_x1 = [P.new_sem(f"x1{i}") for i in range(2)]
        t_c = op("vector", lambda e: e.memset(cst, 0.0))
        barrier()
        free = [()] * 8
        V = {"X_read": None, "G": [None] * 16, "out": [None] * 16, "xW": [None, None], "xW_read": [None, None],
             "xr": {}, "x1s": [None, None], "x1_read": [None, None]}
        NBLK = 32

        def gdense(blk, jp):
            b = 2 + jp % 2
            for i in range(2):
                for k in range(2):
                    t = mm(bank(b)[:, 128 * i:128 * i + 128], kin[:, k, 2 * jp + i, :], xcT[:, k, 128 * blk:128 * blk + 128],
                           k == 0, k == 1, t_kin, *free[b], sig=(i == 1 and k == 1))
            V["G"][jp] = act(G[:, 2 * jp:2 * jp + 2, :], bank(b)[:, 0:256].rearrange("p (a b) -> p a b", a=2), ACT.Gelu,
                             t, V["out"][jp])
            free[b] = (V["G"][jp],)

        def sim_xn(blk):
            n0 = 128 * blk
            for c in range(2):
                V["xn"] = act(xn[:, c, :], xcT[:, c, n0:n0 + 128], ACT.Identity, t_ab, V.get("xn_read"),
                              bias=b_[:, c:c + 1], scale=a_[:, c:c + 1])

        def sim_mm(h):
            for k in range(2):
                t = mm(bank(h), xn[:, k, :], Kc[:, k, 512 * h:512 * h + 512], k == 0, k == 1, V["xn"], t_Kc,
                       *free[h], sig=(k == 1))
            V["xn_read"] = V["sim"] = t

        def topk(blk):
            t1 = V["sim"]
            for g in range(16):
                t1 = mx8(S8[:, g, :], ps[:, 64 * g:64 * g + 64], V["sim"])
                if g % 4 == 3:
                    yield 0.5
            for g in range(16):
                t2 = ix8(I8[:, g, :], S8[:, g, :], ps[:, 64 * g:64 * g + 64], t1)
                if g % 4 == 3:
                    yield 0.5
            t1 = t2
            free[0] = free[1] = (t1,)
            t = cp(I8f, I8, t1)
            t1 = tt(pr, S8[:, 0:8, :].unsqueeze(3).to_broadcast([128, 8, 8, 8]),
                    S8[:, 8:16, :].unsqueeze(2).to_broadcast([128, 8, 8, 8]), ALU.add, t)
            yield 0.5
            prf = pr.rearrange("p a b c -> p a (b c)")
            for h in range(8):
                t1 = mx8(sc[:, h, :], prf[:, h, :], t1)
            t2 = t1
            yield 1
            for h in range(8):
                t1 = ix8(pk[:, h, :], sc[:, h, :], prf[:, h, :], t2)
            t = tt(es, sc, sc[:, :, 0:1].to_broadcast([128, 8, 8]), ALU.subtract, t1)
            t_es = act(es, es, ACT.Exp, t)
            yield 1
            pkf = pk.rearrange("p a b -> p (a b)")
            t1 = ts(ab[:, 0], pkf, 3, None, ALU.logical_shift_right, None, t1)
            t1 = ts(ab[:, 1], pkf, 7, None, ALU.bitwise_and, None, t1)
            t1 = cp(abf, ab, t1)
            io = iota8.unsqueeze(1).to_broadcast([128, 64, 8])
            eqh = eq.rearrange("p (h r) a -> p h r a", h=8)
            for q in range(2):
                t1 = tt(eq, abf[:, q].unsqueeze(2).to_broadcast([128, 64, 8]), io, ALU.is_equal, t1)
                t1 = tt(eqh, eqh, I8f[:, 8 * q:8 * q + 8, :].unsqueeze(2).to_broadcast([128, 8, 8, 8]), ALU.mult, t1)
                t1 = red(ixy[:, q], eq, ALU.add, t1)
                yield 1
            t1 = ts(ge, ixy[:, 1], 32.0, None, ALU.is_ge, None, t1)

            def dup(v):
                return v.unsqueeze(1).to_broadcast([128, 2, 64])
            t1 = stt(Z[:, 0], dup(ixy[:, 0]), 2.0, dup(ge), ALU.mult, ALU.add, t1, V.get("Z_read"))
            t1 = stt(Z[:, 1], dup(ge), -32.0, dup(ixy[:, 1]), ALU.mult, ALU.add, t1)
            t2 = red(ss, es, ALU.add, t_es)
            t2 = recip(ss, ss, t2)
            t2 = tt(es, es, ss.unsqueeze(2).to_broadcast([128, 8, 8]), ALU.mult, t2)
            V["Z"] = cp(Z[:, 2], dup(es.rearrange("p a b -> p (a b)")), t2)

        def ztrans():
            for i in range(3):
                t = tr(bank(0)[:, 128 * i:128 * i + 128], Z[:, i].rearrange("p a b -> p (a b)"), V["Z"], *free[0],
                       sig=(i == 2))
            V["Z_read"] = t
            tp = bank(0)[:, 0:384].rearrange("p (a b) -> p a b", a=3)
            t1 = cp(R3[0:64], tp[0:64, :, 0:64], t)
            t1 = cp(R3[64:128], tp[64:128, :, 64:128], t)
            free[0] = (t1,)
            for i in range(4):
                t2 = ts(xh16[:, i], R3[:, 0], -32.0 * i, None, ALU.add, None, t1)
            t2 = cp(xl16, R3[:, 1], t1)
            t2 = cp(wv[:, 0], R3[:, 2], t1)
            V["sp"] = tt(wv[:, 1], R3[:, 2], wv[:, 0], ALU.subtract, t2)

        def xbuild():
            for i in range(4):
                t3 = tt(X[:, 32 * i:32 * i + 32, :], iot, xh16[:, i].unsqueeze(1).to_broadcast([128, 32, 64]),
                        ALU.is_equal, V["sp"], t_iot, V["X_read"])
                yield 1
            t3 = tt(Y12[:, 1], iot, xl16.unsqueeze(1).to_broadcast([128, 32, 64]), ALU.is_equal, V["sp"])
            yield 1
            for i in range(2):
                t3 = tt(Y12[:, i], Y12[:, 1], wv[:, i].unsqueeze(1).to_broadcast([128, 32, 64]), ALU.mult, t3)
                yield 1
            V["X"] = t3

        def wgroup(n):
            r, gI = n // 2, n % 2
            b = 4 + gI
            p0 = 64 * gI
            for q in range(16):
                tk = 16 * r + q
                for i in range(2):
                    t = mm(bank(b)[:, 32 * q:32 * q + 32], X[p0:p0 + 64, :, tk], Y12[p0:p0 + 64, i, :, tk],
                           i == 0, i == 1, V["X"], *free[b], sig=(q == 15 and i == 1))
            gv = G[:, :, 64 * gI + 16 * r:64 * gI + 16 * r + 16]
            V["A"] = tt(gv, gv, bank(b).rearrange("p (t j) -> p j t", j=32), ALU.mult, t, V["G"][15])
            free[b] = (V["A"],)
            V["X_read"] = t

        def outmm(jp):
            for j in (2 * jp, 2 * jp + 1):
                t = mm(bank(7)[:, 0:256], G[:, j, :], kout[:, j, :], j == 0, j == 31, V["A"], t_kout, *free[7],
                       sig=(j % 2 == 1))
            V["out"][jp] = t

        def x1_add(blk):
            bb = blk % 2
            t_x1 = tt(x1[:, bb], bank(7)[:, 0:256], xr[:, bb], ALU.add, V["out"][15], V["xr"][blk], V["x1s"][bb],
                      V["x1_read"][bb])
            V["x1s"][bb] = dma("sync", x1d[8 * blk:8 * blk + 8].rearrange("t b d -> (t b) d"), x1[:, bb], s_x1[bb], t_x1)
            if blk + 2 < NBLK:
                V["xr"][blk + 2] = dma("sync", xr[:, bb, :], I["xtb"][blk + 2], s_xr[bb], t_x1)
            V["x1"] = t_x1

        def x1_tr(blk):
            bb, n0 = blk % 2, 128 * blk
            for c in range(2):
                t = tr(bank(7)[:, 256 + 128 * c:384 + 128 * c], x1[:, bb, 128 * c:128 * c + 128], V["x1"], sig=(c == 1))
            V["x1_read"][bb] = t
            V["x1T"] = act(xcT[:, :, n0:n0 + 128], bank(7)[:, 256:512].rearrange("p (a b) -> p a b", a=2), ACT.Copy, t)
            free[7] = (V["x1"], V["x1T"])

        def xw(blk, hb):
            n0 = 128 * blk
            for c in range(4):
                for k in range(2):
                    t = mm(bank(7)[:, 128 * c:128 * c + 128], Wx[:, k, 512 * hb + 128 * c:512 * hb + 128 * c + 128],
                           xcT[:, k, n0:n0 + 128], k == 0, k == 1, V["x1T"], *free[7], sig=(k == 1 and c == 3))
            o = xW[:, blk % 2, :, 4 * hb:4 * hb + 4, :]
            t = tt(o, bank(7).rearrange("p (c t b) -> p t c b", c=4, b=16),
                   lb[:, 4 * hb:4 * hb + 4].unsqueeze(1).unsqueeze(3).to_broadcast([128, 8, 4, 16]), ALU.add, t,
                   V["xW_read"][blk % 2])
            free[7] = (t,)
            V["xW"][blk % 2] = t

        L = {"h": None, "c": t_c}

        def split_h(src, n, after):
            t = cp(h3[:, n, :, 0], src, after)
            L["h1"] = t
            t = tt(hr, src, h3[:, n, :, 0], ALU.subtract, t)
            t2 = cp(h3[:, n, :, 1], hr, t)
            L["h3"] = tt(h3[:, n, :, 2], hr, h3[:, n, :, 1], ALU.subtract, t2)

        split_h(h0, 0, t_h0)

        def step(t_):
            n = t_ % 2
            blk = t_ // 8
            o = bank(6)[:, 0:384].rearrange("p (c s) -> p c s", c=8)
            for w in range(3):
                for c in range(8):
                    for k in range(2):
                        mm(o[:, c, 16 * w:48], W3[:, w, k, 128 * c:128 * c + 128],
                           h3[:, n, k, 0:3 - w, :].rearrange("p a b -> p (a b)"), (w, c, k) == (0, 0, 0), False, L["h3"],
                           *free[6])
            t = mm(o[:, :, 0:16], ident, xW[:, blk % 2, t_ % 8], False, True, V["xW"][blk % 2], t_id, sig=True)
            if t_ % 8 == 7:
                V["xW_read"][blk % 2] = t
            t = red(pre, bank(6)[:, 0:384].rearrange("p (c s b) -> p c b s", c=8, s=3),
                    ALU.add, t)
            g = gt[:, n]
            t_g = act(g, pre, ACT.Tanh, t, scale=0.5)
            free[6] = (t,)
            t1 = stt(m1, g[:, 2:4], 1.0, cst, ALU.add, ALU.mult, t_g, L["c"])
            t2 = stt(m2, g[:, 0:2], 1.0, g[:, 6:8], ALU.add, ALU.mult, t_g)
            L["c"] = t1 = stt(cst, m1, 0.5, m2, ALU.mult, ALU.add, t2)
            t3 = act(th, cst, ACT.Tanh, t1, scale=0.5)
            ho = xcT[:, :, 16 * t_:16 * t_ + 16]
            n1 = (t_ + 1) % 2
            L["h1"] = stt(h3[:, n1, :, 0], g[:, 4:6], 1.0, th, ALU.add, ALU.mult, t3)
            t4 = stt(ho, g[:, 4:6], 1.0, th, ALU.add, ALU.mult, t3, V["xW"][blk % 2])
            t4 = tt(hr, ho, h3[:, n1, :, 0], ALU.subtract, t4, L["h1"])
            t5 = cp(h3[:, n1, :, 1], hr, t4)
            L["h3"] = tt(h3[:, n1, :, 2], hr, h3[:, n1, :, 1], ALU.subtract, t5)

        def drive(gen, steps, total):
            at, every = 0.0, total / max(1, len(steps))
            steps = list(steps)
            for w in gen:
                at += w
                while steps and at >= every:
                    at -= every
                    step(steps.pop(0))
            for s_ in steps:
                step(s_)

        def run(gen):
            for _ in gen:
                pass

        for blk in range(2):
            V["xr"][blk] = dma("sync", xr[:, blk, :], I["xtb"][blk], s_xr[blk])
        sim_xn(0)
        sim_mm(0)
        sim_mm(1)
        run(topk(0))
        for jp in range(16):
            gdense(0, jp)
        ztrans()
        run(xbuild())

        def iteration(blk):
            more, past = blk + 1 < NBLK, blk > 0
            tk = topk(blk + 1) if more else iter(())
            xb = xbuild() if more else iter(())
            if past:
                x1_add(blk - 1)
            if more:
                sim_xn(blk + 1)
            for n in range(8):
                wgroup(n)
                yield 0.9
                if more and n < 2:
                    sim_mm(n)
                    yield 1.7
                if past and n == 1:
                    x1_tr(blk - 1)
                if past and n in (3, 5):
                    xw(blk - 1, n // 4)
                    yield 1.8
                if 2 <= n <= 5:
                    next(tk, None)
                    next(tk, None)
            for jp in range(16):
                outmm(jp)
                if more:
                    gdense(blk + 1, jp)
                    next(tk, None)
                    next(tk, None)
                    if jp == ZAT:
                        run(tk)
                        ztrans()
                    if jp > ZAT:
                        next(xb, None)
                        next(xb, None)
                yield 1.74 if more else 0.9
            run(xb)

        ZAT = 9
        for blk in range(NBLK):
            drive(iteration(blk), range(8 * blk - 16, 8 * blk - 8) if blk > 1 else [], 42)
        x1_add(NBLK - 1)
        for t_ in range(8 * NBLK - 16, 8 * NBLK - 8):
            step(t_)
            if t_ % 8 == 1:
                x1_tr(NBLK - 1)
            if t_ % 8 in (3, 5):
                xw(NBLK - 1, t_ % 8 // 4)
        for t_ in range(8 * NBLK - 8, 8 * NBLK):
            step(t_)
        t_x1s = list(V["x1s"])
        barrier()
        if dbg:
            dma("sync", dbg["hT"], xcT, P.new_sem("dbg1"))

        if dbg and dbg.get('upto') == 3:
            return finish()
        arena.at = after_a
        hall = take(32, 256)
        lnp = take(4, 2)
        wqkv, wo = take(2, 768), take(2, 256)
        bqk, msk = take(4), take(8)
        bv, bo = take(256), take(256)
        t_l = [load(lnp, "ln"), load(wqkv, "wqkv"), load(wo, "wo"), load(bqk, "bqk"), load(msk, "mask"), load(bv, "bv"),
               load(bo, "bo")]
        stt6, mv1, rstd = take(32, 6), take(32, 2), take(32)
        free = [()] * 8
        hT = xcT.rearrange("p c (t b) -> p c t b", b=16)
        for m in range(32):
            q, thf = m // 2, m % 2
            b = m % 4
            for c in range(2):
                t = tr(bank(b)[:, 128 * c:128 * c + 128], hT[:, c, 128 * thf:128 * thf + 128, q], *free[b],
                       sig=(c == 1))
            t = act(hall[:, m], bank(b)[:, 0:256], ACT.Copy, t, scale=0.5)
            free[b] = (t,)
            t = op("vector", lambda e, m=m: e.bn_stats(stt6[:, m], hall[:, m]), t)
            t = op("vector", lambda e, m=m: e.bn_aggr(mv1[:, m], stt6[:, m]), t)
        t = act(rstd, mv1[:, :, 1], ACT.Sqrt, t, t_eps, bias=epst)
        t_rstd = recip(rstd, rstd, t)
        barrier()
        arena_m = arena.at
        xh = take(2, 256)
        h1T = take(2, 256)
        qT, kT_ = [take(2, 256) for _ in range(2)], take(2, 256)
        kM = [take(16, 256) for _ in range(2)]
        vv = [take(2, 256) for _ in range(2)]
        NP = 4
        Pp = [take(2, 256) for _ in range(NP)]
        PT = [take(4, 128) for _ in range(NP)]
        nm = [take(2) for _ in range(NP)]
        sm = [take(2, 16) for _ in range(2)]
        rs = take(2, 16)
        on, oT = take(2, 256), take(2, 256)
        free = [()] * 8
        R = {k: None for k in ("xh", "h1T", "kT", "on", "oT")}
        Q = {"q": [None, None], "k": [None, None], "v": [None, None], "S": [None, None], "PV": [None, None],
             "rs": [None, None]}

        def pre(sq):
            i = sq % 2
            for j in range(2):
                m = 2 * sq + j
                t = ts(xh[:, j], hall[:, m], mv1[:, m, 0:1], rstd[:, m:m + 1], ALU.subtract, ALU.mult, t_rstd, R["xh"])
            yield
            for c in range(2):
                for j in range(2):
                    t1 = tr(bank(0)[:, 256 * c + 128 * j:256 * c + 128 * j + 128], xh[:, j, 128 * c:128 * c + 128], t,
                            *free[0], sig=(j == 1))
            R["xh"] = t1
            for c in range(2):
                t_n = act(h1T[:, c], bank(0)[:, 256 * c:256 * c + 256], ACT.Identity, t1, *t_l, R["h1T"],
                          bias=lnp[:, 1, c:c + 1], scale=lnp[:, 0, c:c + 1])
            free[0] = (t_n,)
            yield
            for c in (2, 3, 0, 1):
                for k in range(2):
                    t = mm(bank(0)[:, 0:256], wqkv[:, k, 128 * c:128 * c + 128], h1T[:, k], k == 0, k == 1, t_n,
                           *free[0], sig=(k == 1))
                if c < 2:
                    t = ts(qT[i][:, c], bank(0)[:, 0:256], bqk[:, c:c + 1], 0.25, ALU.add, ALU.mult, t, Q["S"][i])
                else:
                    t = act(kT_[:, c - 2], bank(0)[:, 0:256], ACT.Identity, t, R["kT"], bias=bqk[:, c:c + 1])
                    t_k = t
                free[0] = (t,)
                yield
            Q["q"][i] = t
            for h in range(16):
                t = op("gpsimd", lambda e, h=h: e.tensor_scalar(kM[i][:, h], kT_[:, h // 8], msk[:, h % 8:h % 8 + 1], None,
                                                                ALU.mult), t_k, Q["S"][i])
            Q["k"][i] = R["kT"] = t
            for j in range(2):
                for k in range(2):
                    t = mm(bank(0)[:, 0:256], h1T[:, k, 128 * j:128 * j + 128], wqkv[:, k, 512:768], k == 0, k == 1,
                           *free[0], sig=(k == 1))
                R["h1T"] = t
                t = tt(vv[i][:, j], bank(0)[:, 0:256], bv, ALU.add, t, Q["PV"][i])
                free[0] = (t,)
                yield
            Q["v"][i] = t

        def post(sq):
            i = sq % 2
            t = recip(rs, sm[i], Q["rs"][i])
            for qb in range(2):
                t_on = tt(on[:, qb].rearrange("p (a b) -> p a b", a=16),
                          bank(6 + i)[:, 256 * qb:256 * qb + 256].rearrange("p (a b) -> p a b", a=16),
                          rs[:, qb].unsqueeze(2).to_broadcast([128, 16, 16]), ALU.mult, t, Q["PV"][i], R["on"])
            free[6 + i] = (t_on,)
            yield
            yield
            for c in range(2):
                for j in range(2):
                    t1 = tr(bank(1)[:, 256 * c + 128 * j:256 * c + 128 * j + 128], on[:, j, 128 * c:128 * c + 128], t_on,
                            *free[1], sig=(j == 1))
            R["on"] = t1
            t_oT = act(oT, bank(1).rearrange("p (a b) -> p a b", a=2), ACT.Copy, t1, R["oT"])
            free[1] = (t_oT,)
            yield
            for j in range(2):
                for k in range(2):
                    t = mm(bank(1)[:, 256 * j:256 * j + 256], oT[:, k, 128 * j:128 * j + 128], wo[:, k], k == 0, k == 1,
                           t_oT, *free[1], sig=(k == 1))
            R["oT"] = t
            yield
            for j in range(2):
                m = 2 * sq + j
                t1 = tt(hall[:, m], bank(1)[:, 256 * j:256 * j + 256], hall[:, m], ALU.add, t)
                free[1] = (t1,)
                t1 = tt(hall[:, m], hall[:, m], bo, ALU.add, t1)
                t1 = op("vector", lambda e, m=m: e.bn_stats(stt6[:, m], hall[:, m]), t1)
                op("vector", lambda e, m=m: e.bn_aggr(mv1[:, m], stt6[:, m]), t1)
                yield

        t_e, t_pt, t_tr, t_pv = {}, {}, {}, {}

        def scores(n):
            sq, qb, p_ = n // 16, n // 8 % 2, n % 8
            i, c, b = sq % 2, p_ // 4, 2 + n % 2
            t = mm(bank(b), qT[i][:, c, 128 * qb:128 * qb + 128], kM[i][:, 2 * p_:2 * p_ + 2].rearrange("p a b -> p (a b)"),
                   True, True, Q["q"][i], Q["k"][i], *free[b], sig=True)
            if n % 16 == 15:
                Q["S"][i] = t
            nm_ = nm[n % NP]
            t1 = red(nm_, bank(b).rearrange("p (a b) -> p a b", a=2), ALU.max, t, t_e.get(n - NP), neg=True)
            for hh in range(2):
                t2 = act(Pp[n % NP][:, hh], bank(b)[:, 256 * hh:256 * hh + 256], ACT.Exp, t1, t_tr.get(n - NP),
                         Q["rs_read"][i], bias=nm_[:, hh:hh + 1], acc=sm[i][:, qb, 2 * p_ + hh:2 * p_ + hh + 1])
            free[b] = (t2,)
            t_e[n] = t2
            if n % 16 == 15:
                Q["rs"][i] = t2

        Q["rs_read"] = [None, None]

        def transposes(n):
            b = 4 + n % 2
            for a in range(4):
                t = tr(bank(b)[:, 128 * a:128 * a + 128], Pp[n % NP][:, a // 2, 128 * (a % 2):128 * (a % 2) + 128], t_e[n],
                       *free[b], sig=(a == 3))
            t_tr[n] = t
            t_pt[n] = cp(PT[n % NP], bank(b).rearrange("p (a b) -> p a b", a=4), t, t_pv.get(n - NP))
            free[b] = (t_pt[n],)

        def values(n):
            sq, qb, p_ = n // 16, n // 8 % 2, n % 8
            i = sq % 2
            for a in range(4):
                h, kb = 2 * p_ + a // 2, a % 2
                t = mm(bank(6 + i)[:, 256 * qb + 16 * h:256 * qb + 16 * h + 16], PT[n % NP][:, a],
                       vv[i][:, kb, 16 * h:16 * h + 16], kb == 0, kb == 1, t_pt[n], Q["v"][i], *free[6 + i], sig=(a == 3))
            t_pv[n] = t
            if n % 16 == 15:
                Q["PV"][i] = t

        for _ in pre(0):
            pass
        NU = 16 * 16
        gp, gq = iter(()), iter(())
        for n in range(NU + 3):
            if n < NU:
                if n % 16 == 0:
                    for _ in gp:
                        pass
                    gp = pre(n // 16 + 1) if n // 16 < 15 else iter(())
                scores(n)
            if 2 <= n < NU + 2:
                transposes(n - 2)
            if n >= 3:
                values(n - 3)
                if (n - 3) % 16 == 15:
                    for _ in gq:
                        pass
                    gq = post((n - 3) // 16)
            next(gp, None)
            next(gq, None)
        for _ in gq:
            pass
        barrier()

        if dbg and dbg.get('upto') == 4:
            return finish()
        h2T = xcT
        arena.at = arena_m
        gw, gb_ = take(2, 8), take(8)
        b1, b2 = take(8, 8), take(256)
        t_g = [load(gw, "gate_w"), load(gb_, "gate_b"), load(b1, "b1"), load(b2[0:8], "b2")]
        W1 = [take(2, 1024) for _ in range(2)]
        W2 = [take(8, 256) for _ in range(2)]
        s_w = [P.new_sem(f"ew{i}") for i in range(2)]
        t_ew = {}

        def load_e(e, *after):
            dma("sync", W1[e % 2], I["W1"][:, e], s_w[e % 2], *after)
            t_ew[e] = dma("sync", W2[e % 2], I["W2"][:, e], s_w[e % 2])

        load_e(0)
        load_e(1)
        xh = [take(256) for _ in range(2)]
        lgt, mm8, ii8, ii8f = take(32, 8), take(32, 8), take(32, 8, dt=u32), take(32, 8)
        o1, o2, ew = take(32, 8), take(32, 8), take(32, 8)
        dd, g1, g2 = take(32), take(32), take(32)
        ewT = take(2, 128)
        hid = [take(8, 512) for _ in range(2)]
        free = [()] * 8
        t = act(rstd, mv1[:, :, 1], ACT.Sqrt, bias=epst)
        t_rstd = recip(rstd, rstd, t)
        t_xr2 = [None, None]
        for m in range(32):
            x_ = xh[m % 2]
            t = ts(x_, hall[:, m], mv1[:, m, 0:1], rstd[:, m:m + 1], ALU.subtract, ALU.mult, t_rstd, t_xr2[m % 2])
            b = m % 2
            for c in range(2):
                t1 = tr(bank(b)[:, 128 * c:128 * c + 128], x_[:, 128 * c:128 * c + 128], t, *free[b], sig=(c == 1))
            t_xr2[m % 2] = t1
            for c in range(2):
                t2 = act(h2T[:, c, 128 * m:128 * m + 128], bank(b)[:, 128 * c:128 * c + 128], ACT.Identity, t1,
                         bias=lnp[:, 3, c:c + 1], scale=lnp[:, 2, c:c + 1])
            free[b] = (t2,)
            for k in range(2):
                t = mm(bank(2)[:, 8 * m:8 * m + 8], h2T[:, k, 128 * m:128 * m + 128], gw[:, k], k == 0, k == 1, t2,
                       *t_g, sig=(k == 1))
        t = tt(lgt, bank(2)[:, 0:256].rearrange("p (a b) -> p a b", b=8), gb_.unsqueeze(1).to_broadcast([128, 32, 8]),
               ALU.add, t)
        for m in range(32):
            t1 = mx8(mm8[:, m], lgt[:, m], t)
        for m in range(32):
            t2 = ix8(ii8[:, m], mm8[:, m], lgt[:, m], t1)
        t = cp(ii8f, ii8, t2)
        t1 = tt(dd, mm8[:, :, 1], mm8[:, :, 0], ALU.subtract, t)
        t1 = act(g2, dd, ACT.Exp, t1)
        t1 = ts(g1, g2, 1.0, None, ALU.add, None, t1)
        t1 = recip(g1, g1, t1)
        t1 = tt(g2, g2, g1, ALU.mult, t1)
        io = iota8.unsqueeze(1).to_broadcast([128, 32, 8])
        t2 = tt(o1, ii8f[:, :, 0:1].to_broadcast([128, 32, 8]), io, ALU.is_equal, t)
        t2 = tt(o2, ii8f[:, :, 1:2].to_broadcast([128, 32, 8]), io, ALU.is_equal, t)
        t2 = tt(o1, o1, g1.unsqueeze(2).to_broadcast([128, 32, 8]), ALU.mult, t1, t2)
        t2 = tt(o2, o2, g2.unsqueeze(2).to_broadcast([128, 32, 8]), ALU.mult, t2)
        t_ewt = tt(ew, o1, o2, ALU.add, t2)
        t_er = [None, None]
        for m in range(32):
            b = m % 2
            t = tr(bank(b)[0:8, 0:128], ew[:, m], t_ewt, *free[b], sig=True)
            t = act(ewT[0:8, b], bank(b)[0:8, 0:128], ACT.Copy, t, t_er[b])
            free[b] = (t,)
            t = mm(bank(3 + b)[:, 0:256], ewT[0:8, b], b2[0:8], True, True, t, *free[3 + b], sig=True)
            t_er[b] = t
            t_y = tt(hall[:, m], bank(3 + b)[:, 0:256], hall[:, m], ALU.add, t)
            free[3 + b] = (t_y,)
        barrier()
        free = [()] * 8
        hid_read = [(), ()]
        n = 0
        for e in range(8):
            for s in range(8):
                h_ = hid[s % 2]
                for f in range(8):
                    b = n % 4
                    n += 1
                    for k in range(2):
                        t = mm(bank(b), W1[e % 2][:, k, 128 * f:128 * f + 128], h2T[:, k, 512 * s:512 * s + 512], k == 0,
                               k == 1, t_ew[e], *free[b], sig=(k == 1))
                    if f % 4 != 3:
                        t_r1 = act(h_[:, f], bank(b), ACT.Relu, t, *hid_read[s % 2], bias=b1[:, e, f:f + 1])
                        free[b] = (t_r1,)
                    else:
                        t_r2 = ts(h_[:, f], bank(b), b1[:, e, f:f + 1], 0.0, ALU.add, ALU.max, t, *hid_read[s % 2])
                        free[b] = (t_r2,)
                for j in range(4):
                    m = 4 * s + j
                    b = 4 + j
                    for f in range(8):
                        t = mm(bank(b)[:, 0:256], h_[:, f, 128 * j:128 * j + 128], W2[e % 2][:, f], f == 0, f == 7, t_r1,
                               t_r2, *free[b], sig=(f == 7))
                    t_y = stt(hall[:, m], bank(b)[:, 0:256], ew[:, m, e:e + 1], hall[:, m], ALU.mult, ALU.add, t)
                    free[b] = (t_y,)
                hid_read[s % 2] = (t,)
            if e + 2 < 8:
                load_e(e + 2, t)
        xi = [take(256) for _ in range(4)]
        s_i = [P.new_sem(f"xi{i}") for i in range(4)]
        s_o = [P.new_sem(f"xo{i}") for i in range(4)]
        t_o = [None] * 4
        for m in range(32):
            q, thf = m // 2, m % 2
            i = m % 4
            t = dma("sync", xi[i], x1d[128 * thf:128 * thf + 128, q, :], s_i[i], t_o[i], *t_x1s)
            t = tt(xi[i], xi[i], hall[:, m], ALU.add, t, t_y)
            t_o[i] = dma("sync", out[q, 128 * thf:128 * thf + 128, :], xi[i], s_o[i], t)
        finish()


def layout(i):
    import numpy as np

    def kp(a, k):
        return np.ascontiguousarray(a.reshape(k, 128, *a.shape[1:]).swapaxes(0, 1))

    def rep(a):
        return np.ascontiguousarray(np.broadcast_to(a.reshape(1, -1), (128, a.size)))

    x = i["x"]
    cond = i["cond_1024"]
    cT = kp(np.ascontiguousarray(cond.T), 2)
    d = {
        "xT": kp(np.ascontiguousarray(x.transpose(2, 1, 0)).reshape(256, N), 2),
        "xtb": np.ascontiguousarray(x.transpose(1, 0, 2)).reshape(32, 128, 256),
        "condT": np.ascontiguousarray(np.tile(cT, (1, 1, 8))),
        "h0T": cT,
        "rW": kp(i["L0_cond_router_W"], 4),
        "rb": rep(i["L0_cond_router_bias"]),
        "w1": kp(i["L0_cond_w1"], 2), "w3": kp(i["L0_cond_w3"], 2), "w2": kp(i["L0_cond_w2"], 4),
        "W1e": np.ascontiguousarray(i["L0_cond_W1e"].reshape(8, 2, 128, 256).transpose(2, 0, 1, 3)),
        "W2e": np.ascontiguousarray(i["L0_cond_W2e"].reshape(8, 2, 128, 256).transpose(2, 0, 1, 3)),
        "gamma": np.ascontiguousarray(i["L0_ffn_gamma"].reshape(2, 128).T),
        "beta": np.ascontiguousarray(i["L0_ffn_beta"].reshape(2, 128).T),
        "wq": kp(i["L0_ffn_w_q"], 16),
        "keysT": np.ascontiguousarray(i["L0_ffn_keys"].transpose(3, 2, 0, 1).reshape(128, 16, 64)),
        "kinT": np.ascontiguousarray(i["L0_ffn_key_in"].reshape(128, 32, 2, 128).transpose(3, 2, 1, 0)),
        "kout": i["L0_ffn_key_out"].reshape(128, 32, 256),
        "Wx": kp(i["L1_cond_Wx"], 2), "Wh": kp(i["L1_cond_Wh"], 2),
        "lb": np.ascontiguousarray(i["L1_cond_b"].reshape(8, 128).T),
        "ln": np.ascontiguousarray(np.stack([i["L1_ffn_ln1_g"], i["L1_ffn_ln1_b"], i["L1_ffn_ln2_g"], i["L1_ffn_ln2_b"]])
                                   .reshape(4, 2, 128).transpose(2, 0, 1)),
        "wqkv": kp(i["L1_ffn_w_qkv"], 2),
        "bqk": np.ascontiguousarray(i["L1_ffn_b_qkv"][:512].reshape(4, 128).T),
        "bv": rep(i["L1_ffn_b_qkv"][512:]),
        "wo": kp(i["L1_ffn_w_o"], 2), "bo": rep(i["L1_ffn_b_o"]),
        "gate_w": kp(i["L1_ffn_gate_w"], 2), "gate_b": rep(i["L1_ffn_gate_b"]),
        "W1": np.ascontiguousarray(i["L1_ffn_W1"].reshape(8, 2, 128, 1024).transpose(2, 0, 1, 3)),
        "b1": np.ascontiguousarray(i["L1_ffn_b1"].reshape(8, 8, 128).transpose(2, 0, 1)),
        "W2": np.ascontiguousarray(i["L1_ffn_W2"].reshape(8, 8, 128, 256).transpose(2, 0, 1, 3)),
        "b2": i["L1_ffn_b2"],
        "ident": np.eye(128, dtype=np.float32),
        "iota8": np.tile(np.arange(8, dtype=np.float32), (128, 1)),
        "iota32": np.ascontiguousarray(np.broadcast_to(np.arange(32, dtype=np.float16)[None, :, None], (128, 32, 64))),
        "mask": (np.arange(128)[:, None] // 16 == np.arange(8)[None, :]).astype(np.float32),
    }
    return d


def kernel(**inputs):
    import numpy as np
    import concourse.bacc as bacc
    from concourse.bass_utils import run_bass_kernel_spmd

    nc = bacc.Bacc("TRN2", target_bir_lowering=False, num_devices=1)
    arrays, ins = {}, {}
    for name, a in layout({k: np.asarray(v) for k, v in inputs.items()}).items():
        a = np.ascontiguousarray(a)
        arrays[f"in_{name}"] = a
        ins[name] = nc.dram_tensor(f"in_{name}", a.shape, mybir.dt.from_np(a.dtype), kind="ExternalInput").ap()
    out = nc.dram_tensor("out_0", (NB, T, D), mybir.dt.float32, kind="ExternalOutput").ap()
    build(nc, ins, out)
    r = run_bass_kernel_spmd(nc, [arrays], core_ids=[0])
    return r.results[0]["out_0"]
```

```python
import concourse.bass as bass
from concourse import mybir
from contextlib import ExitStack

NB, T, D = 16, 256, 256
N = NB * T


class Program:

    def __init__(self, nc, ctx):
        self.nc, self.ctx = nc, ctx
        self.q = {k: [] for k in ("tensor", "vector", "scalar", "gpsimd", "sync")}
        self.sem = {k: ctx.enter_context(nc.semaphore("s_" + k)) for k in self.q}
        self.count = {k: 0 for k in self.q}
        self.seen = {k: {} for k in self.q}
        self.nsem = 0
        self.dma_count = {}
        self.dsems = []

    def wait(self, eng, after):
        for tok in after:
            if tok is None:
                continue
            sem, v = tok
            if self.seen[eng].get(id(sem), 0) < v:
                self.seen[eng][id(sem)] = v
                self.q[eng].append(lambda e, sem=sem, v=v: e.wait_ge(sem, v))

    def op(self, eng, f, *after, sig=True):
        self.wait(eng, after)
        if not sig:
            self.q[eng].append(f)
            return None
        self.count[eng] += 1
        s = self.sem[eng]
        self.q[eng].append(lambda e: f(e).then_inc(s, 1))
        return (s, self.count[eng])

    def new_sem(self, name):
        s = self.ctx.enter_context(self.nc.semaphore(name))
        self.dma_count[id(s)] = 0
        self.dsems.append(s)
        return s

    def dma(self, eng, out, in_, sem, *after):
        self.wait(eng, after)
        self.dma_count[id(sem)] += 16
        self.q[eng].append(lambda e: e.dma_start(out, in_).then_inc(sem, 16))
        return (sem, self.dma_count[id(sem)])

    def emit(self, block):
        for name in self.q:
            def body(e, items=self.q[name]):
                for f in items:
                    f(e)
            start = {"tensor": block.tensor, "vector": block.vector, "scalar": block.scalar,
                            "gpsimd": block.gpsimd, "sync": block.sync}[name]
            start(body)


class Arena:
    def __init__(self, t, words):
        self.t, self.words, self.at = t, words, 0

    def take(self, *dims, dt=None):
        n = 1
        for d in dims:
            n *= d
        half = dt is not None and mybir.dt.size(dt) == 2
        w = (n + 1) // 2 if half else n
        w = (w + 7) // 8 * 8
        v = self.t[:, self.at:self.at + w]
        self.at += w
        assert self.at <= self.words, (self.at, self.words)
        if dt is not None:
            v = v.bitcast(dt)
        v = v[:, 0:n]
        if len(dims) == 2:
            v = v.rearrange("p (a b) -> p a b", a=dims[0])
        elif len(dims) == 3:
            v = v.rearrange("p (a b c) -> p a b c", a=dims[0], b=dims[1])
        elif len(dims) == 4:
            v = v.rearrange("p (a b c d) -> p a b c d", a=dims[0], b=dims[1], c=dims[2])
        return v


def build(nc, I, out, dbg=None):
    f32, f16, u32 = mybir.dt.float32, mybir.dt.float16, mybir.dt.uint32
    ALU, ACT, AX = mybir.AluOpType, mybir.ActivationFunctionType, mybir.AxisListType
    WORDS = 53200
    ctx = ExitStack()
    with ctx:
        P = Program(nc, ctx)
        arena = Arena(ctx.enter_context(nc.sbuf_tensor("arena", [128, WORDS], f32)), WORDS)
        ps = ctx.enter_context(nc.psum_tensor("ps", [128, 4096], f32))
        x1d = nc.dram_tensor("x1_scratch", [T, NB, D], f32, kind="Internal").ap()
        x2d = nc.dram_tensor("x2_scratch", [32, 128, D], f32, kind="Internal").ap()
        xsd = nc.dram_tensor("xs_scratch", [9216, D], f32, kind="Internal").ap()
        ysd = nc.dram_tensor("ys_scratch", [9216, D], f32, kind="Internal").ap()
        op, dma = P.op, P.dma
        take = arena.take

        def take_at(at, *dims, dt=None):
            keep, arena.at = arena.at, at
            v = take(*dims, dt=dt)
            arena.at = keep
            return v

        def bank(b, n=1):
            return ps[:, 512 * b:512 * (b + n)]

        free = [()] * 8

        def mm(o, l, r, start, stop, *after, sig=False):
            return op("tensor", lambda e: e.matmul(o, l, r, start=start, stop=stop), *after, sig=sig)

        def tr(o, i, *after, sig=False):
            return op("tensor", lambda e: e.transpose(o, i, ident), *after, sig=sig)

        def act(o, i, fn, *after, bias=0.0, scale=1.0, acc=None):
            if acc is None:
                return op("scalar", lambda e: e.activation(o, i, fn, bias=bias, scale=scale), *after)
            return op("scalar", lambda e: e.activation(o, i, fn, bias=bias, scale=scale, accum_out=acc), *after)

        def tt(o, a, b, alu, *after):
            return op("vector", lambda e: e.tensor_tensor(o, a, b, alu), *after)

        def ts(o, a, s1, s2, o0, o1, *after):
            if o1 is None:
                return op("vector", lambda e: e.tensor_scalar(o, a, s1, None, o0), *after)
            return op("vector", lambda e: e.tensor_scalar(o, a, s1, s2, o0, o1), *after)

        def stt(o, a, s, b, o0, o1, *after):
            return op("vector", lambda e: e.scalar_tensor_tensor(o, a, s, b, o0, o1), *after)

        def cp(o, i, *after):
            return op("vector", lambda e: e.tensor_copy(o, i), *after)

        def red(o, i, alu, *after, neg=False):
            return op("vector", lambda e: e.tensor_reduce(o, i, AX.X, alu, negate=neg), *after)

        def mx8(o, i, *after):
            return op("vector", lambda e: e.max(o, i), *after)

        def ix8(o, m, v, *after):
            return op("vector", lambda e: e.max_index(o, m, v), *after)

        def recip(o, i, *after):
            return op("vector", lambda e: e.reciprocal(o, i), *after)

        def load(tile, name, *after, eng="sync"):
            s = P.new_sem("l_" + name)
            return dma(eng, tile, I[name], s, *after)

        def barrier():
            toks = [(P.sem[k], P.count[k]) for k in P.q if P.count[k]]
            for k in P.q:
                P.wait(k, toks)

        ident = take(128)
        t_id = load(ident, "ident")
        iota8 = take(8)
        t_i8 = load(iota8, "iota8")
        epst = take(1)
        t_eps = op("vector", lambda e: e.memset(epst, 1e-5))
        base = arena.at

        def finish():
            P.wait("sync", [(v, P.dma_count[id(v)]) for v in P.dsems])
            P.emit(ctx.enter_context(nc.Block()))

        NBK = 72
        tri, ones, i72 = take(128), take(128), take(72)
        slot, g12, eid = take(2, 32, dt=u32), take(2, 32), take(72, dt=u32)
        base = arena.at
        xcT = take(2, N)
        after_a = arena.at
        xT, xtok, sh = take(2, N), take(32, 256), take(32, 256)
        zt = take_at(after_a + 16384, 2304)
        t_z = op("gpsimd", lambda e: e.memset(zt, 0.0))
        w1, w3, w2 = take(2, 512), take(2, 512), take(4, 256)
        we_at = arena.at
        W1e, W2e = take(8, 512), take(8, 512)
        silu_s, hs = take(512), take(4, 512)
        scratch = arena.at
        arena.at = base
        cT, rW, rb = take(2, 128), take(4, 8), take(8)
        TL = take(8)
        sg, sl, m8, i8f = take(32, 8), take(32, 8), take(32, 8), take(32, 8)
        i8 = take(32, 8, dt=u32)
        o1, o2, oo = take(32, 8), take(32, 8), take(32, 8)
        cum, tot, pre_ = take(32, 8), take(32, 8), take(32, 8)
        cnt8, cntu, nb8, end8 = take(8), take(8, dt=u32), take(8), take(8)
        cmp_ = take(72, 8)
        sf, eidf = take(2, 32), take(72)
        dn, fl, rr = take(32), take(32), take(32)
        assert arena.at <= after_a
        arena.at = scratch
        t_r = [load(cT, "condT"), load(rW, "rW"), load(rb, "rb")]
        s_xT = [P.new_sem(f"xT{i}") for i in range(8)]
        t_xT = [dma("sync", xT[:, :, 512 * i:512 * i + 512], I["xT"][:, :, 512 * i:512 * i + 512], s_xT[i])
                for i in range(8)]
        t_w = [load(w1, "w1", t_xT[1]), load(w3, "w3"), load(w2, "w2")]
        t_tri = [load(tri, "tri"), load(i72, "iota72")]
        s_z = P.new_sem("zero")
        for i in range(8):
            t_zero = dma("sync", xsd.rearrange("(p n) d -> p (n d)", p=128)[:, 2304 * i:2304 * i + 2304], zt, s_z, t_z,
                         t_xT[7])
        t_tok = dma("sync", xtok, I["xtb"].rearrange("m p d -> p m d"), P.new_sem("xtok"), t_z)
        t_e = [dma("sync", w.rearrange("p e (a b) -> p e a b", a=2), I[n_], P.new_sem(n_), t_tok)
               for n_, w in (("W1e", W1e), ("W2e", W2e))]
        t_one = op("vector", lambda e: e.memset(ones, 1.0))

        def assign(o1, o2, oo, cum, tot, pre_, cnt8, cntu, nb8, end8, cmp_, sf, eidf, t):
            t_oo = tt(oo, o1, o2, ALU.add, t)
            oof = oo.rearrange("p a b -> p (a b)")
            t = mm(bank(6)[:, 0:256], tri, oof, True, True, t_oo, *t_tri, *free[6], sig=True)
            t3 = mm(bank(7)[:, 0:256], ones, oof, True, True, t_oo, t_one, *free[7], sig=True)
            t_cum = cp(cum, bank(6)[:, 0:256].rearrange("p (a b) -> p a b", b=8), t)
            t_tot = cp(tot, bank(7)[:, 0:256].rearrange("p (a b) -> p a b", b=8), t3)
            free[6], free[7] = (t_cum,), (t_tot,)
            for e in range(8):
                t = op("vector", lambda v, e=e: v.tensor_tensor_scan(pre_[:, :, e], ones[:, 0:32], tot[:, :, e], 0.0,
                                                                     ALU.mult, ALU.add), t_tot, t_one)
            t = ts(cnt8, pre_[:, 31, :], 127.0, None, ALU.add, None, t)
            t = cp(cntu, cnt8, t)
            t = ts(cntu, cntu, 7, None, ALU.logical_shift_right, None, t)
            t = cp(nb8, cntu, t)
            t_end = op("vector", lambda v: v.tensor_tensor_scan(end8, ones[:, 0:8], nb8, 0.0, ALU.mult, ALU.add), t)
            t = tt(nb8, end8, nb8, ALU.subtract, t_end)
            t = ts(nb8, nb8, 128.0, None, ALU.mult, None, t)
            t = tt(pre_, pre_, tot, ALU.subtract, t)
            t = tt(cum, cum, pre_, ALU.add, t)
            t = tt(cum, cum, nb8.unsqueeze(1).to_broadcast([128, 32, 8]), ALU.add, t)
            for i, o_ in enumerate((o1, o2)):
                t2 = tt(pre_, cum, o_, ALU.mult, t)
                t = red(sf[:, i], pre_, ALU.add, t2)
            t_slot = cp(slot, sf, t)
            t = tt(cmp_, end8.unsqueeze(1).to_broadcast([128, 72, 8]), i72.unsqueeze(2).to_broadcast([128, 72, 8]),
                   ALU.is_le, t_slot)
            t = red(eidf, cmp_, ALU.add, t)
            t = ts(eidf, eidf, 7.0, None, ALU.min, None, t)
            return t_slot, cp(eid, eidf, t)

        def scatter(name, src, *after):
            s_sc = P.new_sem(name)
            P.wait("gpsimd", after)
            for m in range(32):
                for k in range(2):
                    P.dma_count[id(s_sc)] += 16
                    P.q["gpsimd"].append(lambda e, m=m, k=k: e.indirect_dma_start(
                        xsd, bass.IndirectOffsetOnAxis(ap=slot[:, k, m:m + 1], axis=0), src[:, m], None)
                        .then_inc(s_sc, 16))
            return (s_sc, P.dma_count[id(s_sc)])

        def gather(dst, m, sem, *after):
            P.wait("gpsimd", after)
            for k in range(2):
                P.dma_count[id(sem)] += 16
                P.q["gpsimd"].append(lambda e, k=k: e.indirect_dma_start(
                    dst[:, k], None, ysd, bass.IndirectOffsetOnAxis(ap=slot[:, k, m:m + 1], axis=0)).then_inc(sem, 16))
            return (sem, P.dma_count[id(sem)])

        F = {"hs": None, "w2": None}
        t_sh = {}

        def shared(s):
            x_ = xT[:, :, 512 * s:512 * s + 512]
            for c in range(4):
                u = 2 * (c % 2)
                for w, b in ((w1, u), (w3, u + 1)):
                    for k in range(2):
                        t = mm(bank(b), w[:, k, 128 * c:128 * c + 128], x_[:, k, :], k == 0, k == 1, t_xT[s],
                               *t_w, *free[b], sig=(k == 1))
                    if b == u:
                        t_u = t
                t_si = act(silu_s, bank(u), ACT.Silu, t_u, F["hs"])
                F["hs"] = t_hs = tt(hs[:, c, :], silu_s, bank(u + 1), ALU.mult, t_si, t, F["w2"])
                free[u], free[u + 1] = (t_si,), (t_hs,)
            for j in range(4):
                b = 4 + j // 2
                for c in range(4):
                    t = mm(bank(b)[:, 256 * (j % 2):256 * (j % 2) + 256], hs[:, c, 128 * j:128 * j + 128],
                           w2[:, c, :], c == 0, c == 3, t_hs, *free[b], sig=(c == 3))
                if j % 2:
                    t_sh[s] = act(sh[:, 4 * s + j - 1:4 * s + j + 1, :], bank(b).rearrange("p (a b) -> p a b", a=2),
                                  ACT.Copy, t, t_zero)
                    free[b] = (t_sh[s],)
            F["w2"] = t

        for k in range(2):
            t = mm(bank(7)[:, 0:8], cT[:, k, :], rW[:, 2 + k, :], k == 0, k == 1, *t_r, sig=(k == 1))
        t_TL = cp(TL, bank(7)[:, 0:8], t)
        free[7] = (t_TL,)
        for m in range(32):
            for k in range(2):
                t = mm(bank(6)[:, 8 * m:8 * m + 8], xT[:, k, 128 * m:128 * m + 128], rW[:, k, :], k == 0, k == 1,
                       t_xT[m // 4], sig=(m == 31 and k == 1))
        lg = bank(6)[:, 0:256].rearrange("p (a b) -> p a b", a=32)
        t = tt(sl, lg, TL.unsqueeze(1).to_broadcast([128, 32, 8]), ALU.add, t, t_TL)
        free[6] = (t,)
        t_s = act(sg, sl, ACT.Sigmoid, t)
        t = tt(sl, sg, rb.unsqueeze(1).to_broadcast([128, 32, 8]), ALU.add, t_s)
        for j in range(32):
            t1 = mx8(m8[:, j, :], sl[:, j, :], t)
        for j in range(32):
            t1 = ix8(i8[:, j, :], m8[:, j, :], sl[:, j, :], t1)
        t = cp(i8f, i8, t1)
        io = iota8.unsqueeze(1).to_broadcast([128, 32, 8])
        for k, o_ in enumerate((o1, o2)):
            t1 = tt(o_, i8f[:, :, k:k + 1].to_broadcast([128, 32, 8]), io, ALU.is_equal, t, t_i8)
            t1 = tt(oo, o_, sg, ALU.mult, t1)
            t1 = red(g12[:, k], oo, ALU.add, t1)
        t_sv = t1
        t_slot, t_eid = assign(o1, o2, oo, cum, tot, pre_, cnt8, cntu, nb8, end8, cmp_, sf, eidf, t_sv)
        t = tt(dn, g12[:, 0], g12[:, 1], ALU.add, t_eid)
        t = ts(fl, dn, 1e-9, None, ALU.is_gt, None, t)
        t = ts(rr, dn, 1e-9, None, ALU.add, None, t)
        t = recip(rr, rr, t)
        t = tt(rr, rr, fl, ALU.mult, t)
        t = ts(fl, fl, -0.5, 0.5, ALU.mult, ALU.add, t)
        t = tt(g12, g12, rr.unsqueeze(1).to_broadcast([128, 2, 32]), ALU.mult, t)
        t_g12 = tt(g12, g12, fl.unsqueeze(1).to_broadcast([128, 2, 32]), ALU.add, t)
        t_sc = scatter("scatter0", xtok, t_slot, t_zero, t_tok)

        for s in range(5):
            shared(s)

        NX = 8
        Wa1, Wa2 = [take(2, 256) for _ in range(2)], [take(2, 256) for _ in range(2)]
        xs = [sh[:, 20 + i] for i in range(NX)]
        hb, hid = [take(2, 128) for _ in range(2)], [take(2, 128) for _ in range(2)]
        yb = [take(256) for _ in range(4)]
        s_xs = [P.new_sem(f"axs{i}") for i in range(NX)]
        s_y = [P.new_sem(f"ay{i}") for i in range(4)]
        A = {"xs": {}, "xsr": [None] * NX, "w1": {}, "w2": {}, "w1r": [None, None], "w2r": [None, None],
             "hb": {}, "hbr": [None, None], "hid": {}, "hidr": [None, None], "y": [None] * 4}

        def a_load(n):
            A["xs"][n] = dma("sync", xs[n % NX], xsd[128 * n:128 * n + 128, :], s_xs[n % NX], A["xsr"][n % NX], t_sc)

        def a_head(n):
            i = n % 2
            for c in range(2):
                t = tr(bank(i)[:, 128 * c:128 * c + 128], xs[n % NX][:, 128 * c:128 * c + 128], A["xs"][n], t_id,
                       *free[i], sig=(c == 1))
            A["xsr"][n % NX] = t
            A["hb"][n] = act(hb[i], bank(i)[:, 0:256].rearrange("p (a b) -> p a b", a=2), ACT.Copy, t, A["hbr"][i])
            free[i] = (A["hb"][n],)

        a_reg = {}

        def a_copy1(n):
            i = n % 2

            def first(e):
                a_reg[n] = e.value_load(eid[0:1, n:n + 1], min_val=0, max_val=7)
                return e.tensor_copy(Wa1[i].rearrange("p a b -> p (a b)").unsqueeze(1), W1e[:, bass.ds(a_reg[n], 1)])
            A["w1"][n] = op("vector", first, t_eid, *t_e, A["w1r"][i])

        def a_copy2(n):
            i = n % 2
            A["w2"][n] = op("vector", lambda e: e.tensor_copy(Wa2[i].rearrange("p a b -> p (a b)").unsqueeze(1),
                                                              W2e[:, bass.ds(a_reg[n], 1)]), A["w2r"][i])

        def a_up(n):
            i = n % 2
            for c in range(2):
                for k in range(2):
                    t = mm(bank(2 + i)[:, 128 * c:128 * c + 128], Wa1[i][:, k, 128 * c:128 * c + 128], hb[i][:, k],
                           k == 0, k == 1, A["w1"][n], A["hb"][n], *free[2 + i], sig=(c == 1 and k == 1))
            A["w1r"][i] = A["hbr"][i] = t
            A["hid"][n] = t = act(hid[i], bank(2 + i)[:, 0:256].rearrange("p (a b) -> p a b", a=2), ACT.Gelu, t,
                                  A["hidr"][i])
            free[2 + i] = (t,)

        def a_down(n):
            i = n % 2
            for c in range(2):
                t = mm(bank(4 + i)[:, 0:256], hid[i][:, c], Wa2[i][:, c], c == 0, c == 1, A["hid"][n], A["w2"][n], *free[4 + i],
                       sig=(c == 1))
            A["w2r"][i] = A["hidr"][i] = t
            t = cp(yb[n % 4], bank(4 + i)[:, 0:256], t, A["y"][n % 4])
            free[4 + i] = (t,)
            A["y"][n % 4] = dma("sync", ysd[128 * n:128 * n + 128, :], yb[n % 4], s_y[n % 4], t)

        for n in range(7):
            a_load(n)
        a_copy1(0)
        a_copy2(0)
        a_head(0)
        for n in range(NBK + 1):
            if n + 1 < NBK:
                a_head(n + 1)
                a_copy1(n + 1)
            if n < NBK:
                a_up(n)
            if n:
                a_down(n - 1)
            if n + 1 < NBK:
                a_copy2(n + 1)
            if n + 7 < NBK:
                a_load(n + 7)
        t_ys = list(A["y"])
        arena.at = after_a + 8192
        ya = [take(2, 256) for _ in range(16)]
        assert arena.at == after_a + 16384
        arena.at = we_at
        ya += [take(2, 256) for _ in range(16)]
        assert arena.at == we_at + 8192
        arena.at = WORDS - 256
        st = take(2, 8, 6)
        s_g = [P.new_sem(f"ag{i}") for i in range(8)]
        t_y = {}
        for m in range(32):
            t_y[m // 4] = gather(ya[m], m, s_g[m // 4], *t_ys)
        stats = []

        def combine(s):
            for m in range(4 * s, 4 * s + 4):
                t = stt(sh[:, m], ya[m][:, 0], g12[:, 0, m:m + 1], sh[:, m], ALU.mult, ALU.add, t_sh[s], t_y[s], t_g12)
                t = stt(sh[:, m], ya[m][:, 1], g12[:, 1, m:m + 1], sh[:, m], ALU.mult, ALU.add, t)
            while stats:
                c_, s_, o_, t_ = stats.pop(0)
                F["bn"] = op("vector", lambda e, c_=c_, s_=s_, o_=o_: e.bn_stats(st[:, c_, s_, :], o_), t_)
            for c in range(2):
                b = 6 + c
                for j in range(4):
                    t1 = tr(bank(b)[:, 128 * j:128 * j + 128], sh[:, 4 * s + j, 128 * c:128 * c + 128], t, *free[b],
                            sig=(j == 3))
                o = xcT[:, c, 512 * s:512 * s + 512]
                t_x = act(o, bank(b), ACT.Copy, t1, scale=1.0 / 3.0)
                free[b] = (t_x,)
                stats.append((c, s, o, t_x))

        shared(5)
        shared(6)
        combine(0)
        combine(1)
        shared(7)
        wq, kT, Wh = take_at(after_a, 16, 256), take_at(after_a + 4096, 16, 64), take_at(after_a + 5120, 2, 1024)
        t_k = [load(wq, "wq", F["w2"]), load(kT, "keysT")]
        t_wh = load(Wh, "Wh")
        for s in range(2, 8):
            combine(s)
        for c_, s_, o_, t_ in stats:
            t_bn = op("vector", lambda e, c_=c_, s_=s_, o_=o_: e.bn_stats(st[:, c_, s_, :], o_), t_)
        mv0 = take(2, 2)
        for c in range(2):
            t = op("vector", lambda e, c=c: e.bn_aggr(mv0[:, c, :], st[:, c].rearrange("p a b -> p (a b)")), t_bn)
        barrier()
        kin, kout = take_at(after_a + 8192, 32 * 2 * 128).rearrange("p (k j d) -> p k j d", k=2, j=32), \
            take_at(after_a + 16384, 32, 256)
        arena.at = WORDS - 7360
        ga = take(2)
        ba = take(2)
        gb = [load(ga, "gamma"), load(ba, "beta")]
        mv = take(2, 2)
        t = cp(mv, mv0, t)
        a_, b_ = take(2), take(2)
        t = act(a_, mv[:, :, 1], ACT.Sqrt, t, t_eps, bias=epst)
        t = recip(a_, a_, t)
        t = tt(a_, a_, ga, ALU.mult, t, *gb)
        t = tt(b_, mv[:, :, 0], a_, ALU.mult, t)
        t_ab = tt(b_, ba, b_, ALU.subtract, t)
        if dbg:
            s = P.new_sem("dbg0")
            dma("sync", dbg["xcT"], xcT, s)

        if dbg and dbg.get('upto') == 1:
            return finish()
        bf16 = mybir.dt.bfloat16
        Kc = take(2, 1024)
        Wx = take(2, 1024)
        W3 = take(3, 2, 1024, dt=bf16)
        lb = take(8)
        h0 = take(2, 16)
        wr_ = take_at(after_a + 24576, 2, 1024)
        t_wx = [load(Wx, "Wx"), t_wh, load(lb, "lb"), load(h0, "h0T")]
        t_kin, t_kout = load(kin, "kinT"), load(kout, "kout")
        for c in range(2):
            for g in range(16):
                b = 2 * c + g // 8
                t = mm(bank(b)[:, 64 * (g % 8):64 * (g % 8) + 64], wq[:, g, 128 * c:128 * c + 128], kT[:, g, :],
                       True, True, *t_k, sig=(g % 8 == 7))
                if g % 8 == 7:
                    t_Kc = cp(Kc[:, c, 512 * (g // 8):512 * (g // 8) + 512], bank(b), t)
        t = ts(Wx[:, :, 768:1024], Wx[:, :, 768:1024], 2.0, None, ALU.mult, None, *t_wx)
        t = ts(lb[:, 6:8], lb[:, 6:8], 2.0, None, ALU.mult, None, t)
        t = ts(Wh[:, :, 0:768], Wh[:, :, 0:768], 0.5, None, ALU.mult, None, t)
        t = cp(W3[:, 0], Wh, t)
        t = tt(wr_, Wh, W3[:, 0], ALU.subtract, t)
        t = cp(W3[:, 1], wr_, t)
        t_W3 = tt(W3[:, 2], wr_, W3[:, 1], ALU.subtract, t)
        t_h0 = ts(h0, h0, 2.0, None, ALU.mult, None, t)
        barrier()
        arena.at = after_a
        iot = take(32, 64, dt=f16)
        t_iot = load(iot, "iota32")
        G = take(32, 128)
        Y12 = take(2, 32, 64, dt=f16)
        pr, eq = take(8, 8, 8), take(64, 8)
        assert arena.at == after_a + 8192
        arena.at = after_a + 24576
        X = take(128, 64, dt=f16)
        xn = take(2, 128)
        S8, I8, I8f = take(16, 8), take(16, 8, dt=u32), take(16, 8)
        sc, pk = take(8, 8), take(8, 8, dt=u32)
        ab, abf = take(2, 64, dt=u32), take(2, 64)
        ixy = take(2, 64)
        ge, es, ss = take(64), take(8, 8), take(8)
        Z = take(3, 2, 64)
        R3 = take(3, 64)
        xh16 = take(4, 64, dt=f16)
        xl16, wv = take(64, dt=f16), take(2, 64, dt=f16)
        xr = take(2, 256)
        x1 = take(2, 256)
        xW = take(2, 8, 8, 16)
        cst, gt, pre = take(2, 16), take(2, 8, 16), take(8, 16)
        m1, m2, th, hr = take(2, 16), take(2, 16), take(2, 16), take(2, 16)
        h3 = take(2, 2, 3, 16, dt=bf16)
        assert arena.at <= WORDS - 7360
        s_xr = [P.new_sem(f"xr{i}") for i in range(2)]
        s_x1 = [P.new_sem(f"x1{i}") for i in range(2)]
        t_c = op("vector", lambda e: e.memset(cst, 0.0))
        barrier()
        free = [()] * 8
        V = {"X_read": None, "G": [None] * 16, "out": [None] * 16, "xW": [None, None], "xW_read": [None, None],
             "xr": {}, "x1s": [None, None], "x1_read": [None, None]}
        NBLK = 32

        def gdense(blk, jp):
            b = 2 + jp % 2
            for i in range(2):
                for k in range(2):
                    t = mm(bank(b)[:, 128 * i:128 * i + 128], kin[:, k, 2 * jp + i, :], xcT[:, k, 128 * blk:128 * blk + 128],
                           k == 0, k == 1, t_kin, *free[b], sig=(i == 1 and k == 1))
            V["G"][jp] = act(G[:, 2 * jp:2 * jp + 2, :], bank(b)[:, 0:256].rearrange("p (a b) -> p a b", a=2), ACT.Gelu,
                             t, V["out"][jp])
            free[b] = (V["G"][jp],)

        def sim_xn(blk):
            n0 = 128 * blk
            for c in range(2):
                V["xn"] = act(xn[:, c, :], xcT[:, c, n0:n0 + 128], ACT.Identity, t_ab, V.get("xn_read"),
                              bias=b_[:, c:c + 1], scale=a_[:, c:c + 1])

        def sim_mm(h):
            for k in range(2):
                t = mm(bank(h), xn[:, k, :], Kc[:, k, 512 * h:512 * h + 512], k == 0, k == 1, V["xn"], t_Kc,
                       *free[h], sig=(k == 1))
            V["xn_read"] = V["sim"] = t

        def topk(blk):
            t1 = V["sim"]
            for g in range(16):
                t1 = mx8(S8[:, g, :], ps[:, 64 * g:64 * g + 64], V["sim"])
                if g % 4 == 3:
                    yield 0.5
            for g in range(16):
                t2 = ix8(I8[:, g, :], S8[:, g, :], ps[:, 64 * g:64 * g + 64], t1)
                if g % 4 == 3:
                    yield 0.5
            t1 = t2
            free[0] = free[1] = (t1,)
            t = cp(I8f, I8, t1)
            t1 = tt(pr, S8[:, 0:8, :].unsqueeze(3).to_broadcast([128, 8, 8, 8]),
                    S8[:, 8:16, :].unsqueeze(2).to_broadcast([128, 8, 8, 8]), ALU.add, t)
            yield 0.5
            prf = pr.rearrange("p a b c -> p a (b c)")
            for h in range(8):
                t1 = mx8(sc[:, h, :], prf[:, h, :], t1)
            t2 = t1
            yield 1
            for h in range(8):
                t1 = ix8(pk[:, h, :], sc[:, h, :], prf[:, h, :], t2)
            t = tt(es, sc, sc[:, :, 0:1].to_broadcast([128, 8, 8]), ALU.subtract, t1)
            t_es = act(es, es, ACT.Exp, t)
            yield 1
            pkf = pk.rearrange("p a b -> p (a b)")
            t1 = ts(ab[:, 0], pkf, 3, None, ALU.logical_shift_right, None, t1)
            t1 = ts(ab[:, 1], pkf, 7, None, ALU.bitwise_and, None, t1)
            t1 = cp(abf, ab, t1)
            io = iota8.unsqueeze(1).to_broadcast([128, 64, 8])
            eqh = eq.rearrange("p (h r) a -> p h r a", h=8)
            for q in range(2):
                t1 = tt(eq, abf[:, q].unsqueeze(2).to_broadcast([128, 64, 8]), io, ALU.is_equal, t1)
                t1 = tt(eqh, eqh, I8f[:, 8 * q:8 * q + 8, :].unsqueeze(2).to_broadcast([128, 8, 8, 8]), ALU.mult, t1)
                t1 = red(ixy[:, q], eq, ALU.add, t1)
                yield 1
            t1 = ts(ge, ixy[:, 1], 32.0, None, ALU.is_ge, None, t1)

            def dup(v):
                return v.unsqueeze(1).to_broadcast([128, 2, 64])
            t1 = stt(Z[:, 0], dup(ixy[:, 0]), 2.0, dup(ge), ALU.mult, ALU.add, t1, V.get("Z_read"))
            t1 = stt(Z[:, 1], dup(ge), -32.0, dup(ixy[:, 1]), ALU.mult, ALU.add, t1)
            t2 = red(ss, es, ALU.add, t_es)
            t2 = recip(ss, ss, t2)
            t2 = tt(es, es, ss.unsqueeze(2).to_broadcast([128, 8, 8]), ALU.mult, t2)
            V["Z"] = cp(Z[:, 2], dup(es.rearrange("p a b -> p (a b)")), t2)

        def ztrans():
            for i in range(3):
                t = tr(bank(0)[:, 128 * i:128 * i + 128], Z[:, i].rearrange("p a b -> p (a b)"), V["Z"], *free[0],
                       sig=(i == 2))
            V["Z_read"] = t
            tp = bank(0)[:, 0:384].rearrange("p (a b) -> p a b", a=3)
            t1 = cp(R3[0:64], tp[0:64, :, 0:64], t)
            t1 = cp(R3[64:128], tp[64:128, :, 64:128], t)
            free[0] = (t1,)
            for i in range(4):
                t2 = ts(xh16[:, i], R3[:, 0], -32.0 * i, None, ALU.add, None, t1)
            t2 = cp(xl16, R3[:, 1], t1)
            t2 = cp(wv[:, 0], R3[:, 2], t1)
            V["sp"] = tt(wv[:, 1], R3[:, 2], wv[:, 0], ALU.subtract, t2)

        def xbuild():
            for i in range(4):
                t3 = tt(X[:, 32 * i:32 * i + 32, :], iot, xh16[:, i].unsqueeze(1).to_broadcast([128, 32, 64]),
                        ALU.is_equal, V["sp"], t_iot, V["X_read"])
                yield 1
            t3 = tt(Y12[:, 1], iot, xl16.unsqueeze(1).to_broadcast([128, 32, 64]), ALU.is_equal, V["sp"])
            yield 1
            for i in range(2):
                t3 = tt(Y12[:, i], Y12[:, 1], wv[:, i].unsqueeze(1).to_broadcast([128, 32, 64]), ALU.mult, t3)
                yield 1
            V["X"] = t3

        def wgroup(n):
            r, gI = n // 2, n % 2
            b = (4, 5)[n % 2]
            p0 = 64 * gI
            for q in range(16):
                tk = 16 * r + q
                for i in range(2):
                    t = mm(bank(b)[:, 32 * q:32 * q + 32], X[p0:p0 + 64, :, tk], Y12[p0:p0 + 64, i, :, tk],
                           i == 0, i == 1, V["X"], *free[b], sig=(q == 15 and i == 1))
            gv = G[:, :, 64 * gI + 16 * r:64 * gI + 16 * r + 16]
            V["A"] = tt(gv, gv, bank(b).rearrange("p (t j) -> p j t", j=32), ALU.mult, t, V["G"][15])
            free[b] = (V["A"],)
            V["X_read"] = t

        def outmm(jp):
            for j in (2 * jp, 2 * jp + 1):
                t = mm(bank(7)[:, 0:256], G[:, j, :], kout[:, j, :], j == 0, j == 31, V["A"], t_kout, *free[7],
                       sig=(j % 2 == 1))
            V["out"][jp] = t

        def x1_add(blk):
            bb = blk % 2
            t_x1 = tt(x1[:, bb], bank(7)[:, 0:256], xr[:, bb], ALU.add, V["out"][15], V["xr"][blk], V["x1s"][bb],
                      V["x1_read"][bb])
            V["x1s"][bb] = dma("sync", x1d[8 * blk:8 * blk + 8].rearrange("t b d -> (t b) d"), x1[:, bb], s_x1[bb], t_x1)
            if blk + 2 < NBLK:
                V["xr"][blk + 2] = dma("sync", xr[:, bb, :], I["xtb"][blk + 2], s_xr[bb], t_x1)
            V["x1"] = t_x1

        def x1_tr(blk):
            bb, n0 = blk % 2, 128 * blk
            for c in range(2):
                t = tr(bank(7)[:, 256 + 128 * c:384 + 128 * c], x1[:, bb, 128 * c:128 * c + 128], V["x1"], sig=(c == 1))
            V["x1_read"][bb] = t
            V["x1T"] = act(xcT[:, :, n0:n0 + 128], bank(7)[:, 256:512].rearrange("p (a b) -> p a b", a=2), ACT.Copy, t)
            free[7] = (V["x1"], V["x1T"])

        def xw(blk, hb):
            n0 = 128 * blk
            for c in range(4):
                for k in range(2):
                    t = mm(bank(7)[:, 128 * c:128 * c + 128], Wx[:, k, 512 * hb + 128 * c:512 * hb + 128 * c + 128],
                           xcT[:, k, n0:n0 + 128], k == 0, k == 1, V["x1T"], *free[7], sig=(k == 1 and c == 3))
            o = xW[:, blk % 2, :, 4 * hb:4 * hb + 4, :]
            t = tt(o, bank(7).rearrange("p (c t b) -> p t c b", c=4, b=16),
                   lb[:, 4 * hb:4 * hb + 4].unsqueeze(1).unsqueeze(3).to_broadcast([128, 8, 4, 16]), ALU.add, t,
                   V["xW_read"][blk % 2])
            free[7] = (t,)
            V["xW"][blk % 2] = t

        L = {"h": None, "c": t_c}

        def split_h(src, n, after):
            t = cp(h3[:, n, :, 0], src, after)
            L["h1"] = t
            t = tt(hr, src, h3[:, n, :, 0], ALU.subtract, t)
            t2 = cp(h3[:, n, :, 1], hr, t)
            L["h3"] = tt(h3[:, n, :, 2], hr, h3[:, n, :, 1], ALU.subtract, t2)

        split_h(h0, 0, t_h0)

        def step(t_):
            if t_ < 0:
                return
            n = t_ % 2
            blk = t_ // 8
            o = bank(6)[:, 0:384].rearrange("p (c s) -> p c s", c=8)
            for w in range(3):
                for c in range(8):
                    for k in range(2):
                        mm(o[:, c, 16 * w:48], W3[:, w, k, 128 * c:128 * c + 128],
                           h3[:, n, k, 0:3 - w, :].rearrange("p a b -> p (a b)"), (w, c, k) == (0, 0, 0), False, L["h3"],
                           *free[6])
            t = mm(o[:, :, 0:16], ident, xW[:, blk % 2, t_ % 8], False, True, V["xW"][blk % 2], t_id, sig=True)
            if t_ % 8 == 7:
                V["xW_read"][blk % 2] = t
            t = red(pre, bank(6)[:, 0:384].rearrange("p (c s b) -> p c b s", c=8, s=3),
                    ALU.add, t)
            g = gt[:, n]
            t_g = act(g, pre, ACT.Tanh, t, scale=0.5)
            free[6] = (t,)
            t1 = stt(m1, g[:, 2:4], 1.0, cst, ALU.add, ALU.mult, t_g, L["c"])
            t2 = stt(m2, g[:, 0:2], 1.0, g[:, 6:8], ALU.add, ALU.mult, t_g)
            L["c"] = t1 = stt(cst, m1, 0.5, m2, ALU.mult, ALU.add, t2)
            t3 = act(th, cst, ACT.Tanh, t1, scale=0.5)
            ho = xcT[:, :, 16 * t_:16 * t_ + 16]
            n1 = (t_ + 1) % 2
            L["h1"] = stt(h3[:, n1, :, 0], g[:, 4:6], 1.0, th, ALU.add, ALU.mult, t3)
            t4 = stt(ho, g[:, 4:6], 1.0, th, ALU.add, ALU.mult, t3, V["xW"][blk % 2])
            t4 = tt(hr, ho, h3[:, n1, :, 0], ALU.subtract, t4, L["h1"])
            t5 = cp(h3[:, n1, :, 1], hr, t4)
            L["h3"] = tt(h3[:, n1, :, 2], hr, h3[:, n1, :, 1], ALU.subtract, t5)

        def drive(gen, steps, total):
            at, every = 0.0, total / max(1, len(steps))
            steps = list(steps)
            for w in gen:
                at += w
                while steps and at >= every:
                    at -= every
                    step(steps.pop(0))
            for s_ in steps:
                step(s_)

        def run(gen):
            for _ in gen:
                pass

        for blk in range(2):
            V["xr"][blk] = dma("sync", xr[:, blk, :], I["xtb"][blk], s_xr[blk])
        sim_xn(0)
        sim_mm(0)
        sim_mm(1)
        sim_xn(1)
        run(topk(0))
        for jp in range(16):
            gdense(0, jp)
        ztrans()
        run(xbuild())

        def iteration(blk):
            more, past = blk + 1 < NBLK, blk > 0
            tk = topk(blk + 1) if more else iter(())
            xb = xbuild() if more else iter(())
            if past:
                x1_add(blk - 1)
            for n in range(8):
                wgroup(n)
                yield 0.9
                if more and n < 2:
                    sim_mm(n)
                    yield 1.7
                if past and n == 1:
                    x1_tr(blk - 1)
                if past and n in XWN:
                    xw(blk - 1, n // 5)
                    yield 1.8
                for _ in range(TKN[n]):
                    next(tk, None)
            for jp in range(16):
                outmm(jp)
                if more:
                    gdense(blk + 1, jp)
                    for _ in range(TKJ):
                        next(tk, None)
                    if jp == ZAT:
                        run(tk)
                        ztrans()
                    if jp > ZAT:
                        for _ in range(XBJ):
                            next(xb, None)
                if jp == 12 and blk + 2 < NBLK:
                    sim_xn(blk + 2)
                yield 1.74 if more else 0.9
            run(xb)

        XWN, TKJ, XBJ = (3, 7), 1, 1
        ZAT, LAG, TKN = 8, 2, (0, 0, 2, 2, 2, 2, 0, 0)
        for blk in range(NBLK):
            drive(iteration(blk), range(8 * blk - 8 - LAG, 8 * blk - LAG) if blk else [], 41 if blk < NBLK - 1 else 25)
        x1_add(NBLK - 1)
        x1_tr(NBLK - 1)
        xw(NBLK - 1, 0)
        xw(NBLK - 1, 1)
        for t_ in range(8 * NBLK - 8 - LAG, 8 * NBLK):
            step(t_)
        t_x1s = list(V["x1s"])
        barrier()
        if dbg:
            dma("sync", dbg["hT"], xcT, P.new_sem("dbg1"))

        if dbg and dbg.get('upto') == 3:
            return finish()
        arena.at = after_a
        hall = take(32, 256)
        lnp = take(4, 2)
        qkv_at = arena.at
        wqkv, wo = take(2, 768), take(2, 256)
        bqk, msk = take(4), take(8)
        bv, bo = take(256), take(256)
        t_l = [load(lnp, "ln"), load(wqkv, "wqkv"), load(wo, "wo"), load(bqk, "bqk"), load(msk, "mask"), load(bv, "bv"),
               load(bo, "bo")]
        gw, gb_ = take(2, 8), take(8)
        t_g = [load(gw, "gate_w"), load(gb_, "gate_b")]
        lgt, mm8, ii8 = take(32, 8), take(32, 8), take(32, 8, dt=u32)
        wr_at = arena.at
        stt6, mv1, rstd = take(32, 6), take(32, 2), take(32)
        free = [()] * 8
        hT = xcT.rearrange("p c (t b) -> p c t b", b=16)

        def norm1(m, b):
            q, thf = m // 2, m % 2
            for c in range(2):
                t = tr(bank(b)[:, 128 * c:128 * c + 128], hT[:, c, 128 * thf:128 * thf + 128, q], *free[b],
                       sig=(c == 1))
            t = act(hall[:, m], bank(b)[:, 0:256], ACT.Copy, t, scale=0.5)
            free[b] = (t,)
            t = op("vector", lambda e, m=m: e.bn_stats(stt6[:, m], hall[:, m]), t)
            return op("vector", lambda e, m=m: e.bn_aggr(mv1[:, m], stt6[:, m]), t)

        def norm1_end(m0, m1, t):
            t = act(rstd[:, m0:m1], mv1[:, m0:m1, 1], ACT.Sqrt, t, t_eps, bias=epst)
            return recip(rstd[:, m0:m1], rstd[:, m0:m1], t)

        def norm1_rest():
            for m in range(4, 32):
                t = norm1(m, 1)
                if m % 2:
                    yield
            Q["rstd"] = norm1_end(4, 32, t)
            yield

        for m in range(4):
            t = norm1(m, m)
        t_rstd = norm1_end(0, 4, t)
        barrier()
        arena_m = arena.at
        xh = take(2, 256)
        h1T = take(2, 256)
        qT, kT_ = [take(2, 256) for _ in range(2)], take(2, 256)
        kM = [take(16, 256) for _ in range(2)]
        vv = [take(2, 256) for _ in range(2)]
        NP, PL = 7, 5
        Pp = [take(2, 256) for _ in range(NP)]
        PT = [take(4, 128) for _ in range(NP)]
        nm = [take(2) for _ in range(NP)]
        sm = [take(2, 16) for _ in range(2)]
        rs = take(2, 16)
        on, oT = take(2, 256), take(2, 256)
        h2 = take(2, 256)
        NXB = 4
        xb = [take(256) for _ in range(NXB)]
        s_i = [P.new_sem(f"xi{i}") for i in range(NXB)]
        s_o = [P.new_sem(f"xo{i}") for i in range(NXB)]
        t_xo = [None] * NXB
        free = [()] * 8
        R = {k: None for k in ("xh", "h1T", "kT", "on", "oT", "h2")}
        Q = {"q": [None, None], "k": [None, None], "v": [None, None], "S": [None, None], "PV": [None, None],
             "rs": [None, None], "rstd": t_rstd, "hb": {}}

        def pre(sq):
            i = sq % 2
            for j in range(2):
                m = 2 * sq + j
                t = ts(xh[:, j], hall[:, m], mv1[:, m, 0:1], rstd[:, m:m + 1], ALU.subtract, ALU.mult, Q["rstd"], R["xh"])
            for m in (2 * sq, 2 * sq + 1):
                Q["hb"][m] = op("gpsimd", lambda e, m=m: e.tensor_tensor(hall[:, m], hall[:, m], bo, ALU.add), t, *t_l)
            yield
            for c in range(2):
                for j in range(2):
                    t1 = tr(bank(0)[:, 256 * c + 128 * j:256 * c + 128 * j + 128], xh[:, j, 128 * c:128 * c + 128], t,
                            *free[0], sig=(j == 1))
            R["xh"] = t1
            for c in range(2):
                t_n = act(h1T[:, c], bank(0)[:, 256 * c:256 * c + 256], ACT.Identity, t1, *t_l, R["h1T"],
                          bias=lnp[:, 1, c:c + 1], scale=lnp[:, 0, c:c + 1])
            free[0] = (t_n,)
            yield
            for c in (2, 3, 0, 1):
                for k in range(2):
                    t = mm(bank(0)[:, 0:256], wqkv[:, k, 128 * c:128 * c + 128], h1T[:, k], k == 0, k == 1, t_n,
                           *free[0], sig=(k == 1))
                if c < 2:
                    t = ts(qT[i][:, c], bank(0)[:, 0:256], bqk[:, c:c + 1], 0.25, ALU.add, ALU.mult, t, Q["S"][i])
                else:
                    t = act(kT_[:, c - 2], bank(0)[:, 0:256], ACT.Identity, t, R["kT"], bias=bqk[:, c:c + 1])
                    t_k = t
                free[0] = (t,)
                yield
            Q["q"][i] = t
            for h in range(16):
                t = op("gpsimd", lambda e, h=h: e.tensor_scalar(kM[i][:, h], kT_[:, h // 8], msk[:, h % 8:h % 8 + 1], None,
                                                                ALU.mult), t_k, Q["S"][i])
            Q["k"][i] = R["kT"] = t
            for j in range(2):
                for k in range(2):
                    t = mm(bank(0)[:, 0:256], h1T[:, k, 128 * j:128 * j + 128], wqkv[:, k, 512:768], k == 0, k == 1,
                           *free[0], sig=(k == 1))
                R["h1T"] = t
                t = tt(vv[i][:, j], bank(0)[:, 0:256], bv, ALU.add, t, Q["PV"][i])
                free[0] = (t,)
                yield
            Q["v"][i] = t

        def post(sq):
            i = sq % 2
            t = recip(rs, sm[i], Q["rs"][i])
            for qb in range(2):
                t_on = tt(on[:, qb].rearrange("p (a b) -> p a b", a=16),
                          bank(6 + i)[:, 256 * qb:256 * qb + 256].rearrange("p (a b) -> p a b", a=16),
                          rs[:, qb].unsqueeze(2).to_broadcast([128, 16, 16]), ALU.mult, t, Q["PV"][i], R["on"])
            free[6 + i] = (t_on,)
            yield
            yield
            for c in range(2):
                for j in range(2):
                    t1 = tr(bank(1)[:, 256 * c + 128 * j:256 * c + 128 * j + 128], on[:, j, 128 * c:128 * c + 128], t_on,
                            *free[1], sig=(j == 1))
            R["on"] = t1
            t_oT = act(oT, bank(1).rearrange("p (a b) -> p a b", a=2), ACT.Copy, t1, R["oT"])
            free[1] = (t_oT,)
            yield
            for j in range(2):
                for k in range(2):
                    t = mm(bank(1)[:, 256 * j:256 * j + 256], oT[:, k, 128 * j:128 * j + 128], wo[:, k], k == 0, k == 1,
                           t_oT, *free[1], sig=(k == 1))
            R["oT"] = t
            yield
            t_x = []
            for j in range(2):
                x = (2 * sq + j) % NXB
                t_x.append(dma("sync", xb[x], x1d[128 * j:128 * j + 128, sq, :], s_i[x], t_xo[x], *t_x1s))
            for j in range(2):
                m = 2 * sq + j
                x = m % NXB
                t1 = tt(hall[:, m], bank(1)[:, 256 * j:256 * j + 256], hall[:, m], ALU.add, t, Q["hb"][m])
                free[1] = (t1,)
                t2 = op("vector", lambda e, m=m: e.bn_stats(stt6[:, m], hall[:, m]), t1)
                t3 = op("gpsimd", lambda e, m=m, x=x: e.tensor_tensor(xb[x], xb[x], hall[:, m], ALU.add), t1, t_x[j])
                t_xo[x] = dma("sync", x2d[m], xb[x], s_o[x], t3)
                t1 = op("vector", lambda e, m=m: e.bn_aggr(mv1[:, m], stt6[:, m]), t2)
                yield
            m = 2 * sq
            t1 = act(rstd[:, m:m + 2], mv1[:, m:m + 2, 1], ACT.Sqrt, t1, bias=epst)
            t1 = recip(rstd[:, m:m + 2], rstd[:, m:m + 2], t1)
            for m in (2 * sq, 2 * sq + 1):
                t2 = ts(hall[:, m], hall[:, m], mv1[:, m, 0:1], rstd[:, m:m + 1], ALU.subtract, ALU.mult, t1, t3)
            yield
            yield
            for c in range(2):
                for j in range(2):
                    t = tr(bank(1)[:, 256 * c + 128 * j:256 * c + 128 * j + 128], hall[:, 2 * sq + j, 128 * c:128 * c + 128],
                           t2, *free[1], sig=(j == 1))
            for c in range(2):
                t1 = act(h2[:, c], bank(1)[:, 256 * c:256 * c + 256], ACT.Identity, t, R["h2"],
                         bias=lnp[:, 3, c:c + 1], scale=lnp[:, 2, c:c + 1])
            free[1] = (t1,)
            yield
            for j in range(2):
                for k in range(2):
                    t = mm(bank(1)[:, 8 * j:8 * j + 8], h2[:, k, 128 * j:128 * j + 128], gw[:, k], k == 0, k == 1, t1, *t_g,
                           *free[1], sig=(j == 1 and k == 1))
            R["h2"] = t
            t = tt(lgt[:, 2 * sq:2 * sq + 2], bank(1)[:, 0:16].rearrange("p (a b) -> p a b", b=8),
                   gb_.unsqueeze(1).to_broadcast([128, 2, 8]), ALU.add, t)
            free[1] = (t,)
            for m in (2 * sq, 2 * sq + 1):
                t1 = mx8(mm8[:, m], lgt[:, m], t)
            for m in (2 * sq, 2 * sq + 1):
                Q["lg"] = ix8(ii8[:, m], mm8[:, m], lgt[:, m], t1)
            yield

        t_e, t_pt, t_tr, t_pv = {}, {}, {}, {}

        def scores(n):
            sq, qb, p_ = n // 16, n // 8 % 2, n % 8
            i, c, b = sq % 2, p_ // 4, 2 + n % 2
            t = mm(bank(b), qT[i][:, c, 128 * qb:128 * qb + 128], kM[i][:, 2 * p_:2 * p_ + 2].rearrange("p a b -> p (a b)"),
                   True, True, Q["q"][i], Q["k"][i], *free[b], sig=True)
            if n % 16 == 15:
                Q["S"][i] = t
            nm_ = nm[n % NP]
            t1 = red(nm_, bank(b).rearrange("p (a b) -> p a b", a=2), ALU.max, t, t_e.get(n - NP), neg=True)
            for hh in range(2):
                t2 = act(Pp[n % NP][:, hh], bank(b)[:, 256 * hh:256 * hh + 256], ACT.Exp, t1, t_tr.get(n - NP),
                         Q["rs_read"][i], bias=nm_[:, hh:hh + 1], acc=sm[i][:, qb, 2 * p_ + hh:2 * p_ + hh + 1])
            free[b] = (t2,)
            t_e[n] = t2
            if n % 16 == 15:
                Q["rs"][i] = t2

        Q["rs_read"] = [None, None]

        def transposes(n):
            b = 4 + n % 2
            for a in range(4):
                t = tr(bank(b)[:, 128 * a:128 * a + 128], Pp[n % NP][:, a // 2, 128 * (a % 2):128 * (a % 2) + 128], t_e[n],
                       *free[b], sig=(a == 3))
            t_tr[n] = t
            t_pt[n] = cp(PT[n % NP], bank(b).rearrange("p (a b) -> p a b", a=4), t, t_pv.get(n - NP))
            free[b] = (t_pt[n],)

        def values(n):
            sq, qb, p_ = n // 16, n // 8 % 2, n % 8
            i = sq % 2
            for a in range(4):
                h, kb = 2 * p_ + a // 2, a % 2
                t = mm(bank(6 + i)[:, 256 * qb + 16 * h:256 * qb + 16 * h + 16], PT[n % NP][:, a],
                       vv[i][:, kb, 16 * h:16 * h + 16], kb == 0, kb == 1, t_pt[n], Q["v"][i], *free[6 + i], sig=(a == 3))
            t_pv[n] = t
            if n % 16 == 15:
                Q["PV"][i] = t

        for _ in pre(0):
            pass
        NU = 16 * 16
        gp, gq = iter(()), iter(())
        gn = norm1_rest()
        for n in range(NU + PL):
            next(gn, None)
            if n < NU:
                if n % 16 == 0:
                    for _ in gp:
                        pass
                    gp = pre(n // 16 + 1) if n // 16 < 15 else iter(())
                scores(n)
            if 2 <= n < NU + 2:
                transposes(n - 2)
            if n >= PL:
                values(n - PL)
                if (n - PL) % 16 == 15:
                    for _ in gq:
                        pass
                    gq = post((n - PL) // 16)
            next(gp, None)
            next(gq, None)
        for _ in gq:
            pass
        t_lg = Q["lg"]
        t_x2 = list(t_xo)
        for k in P.q:
            P.wait(k, t_x2)
        barrier()

        if dbg and dbg.get('upto') == 4:
            return finish()
        arena_m = wr_at
        Wr1, Wr2 = take_at(arena_m, 8, 2048), take_at(arena_m + 16384, 8, 2048)
        s_w = [P.new_sem(f"ew{i}") for i in range(2)]
        for e in range(8):
            t_w1 = dma("sync", Wr1[:, e], I["W1"][:, e].rearrange("p a b -> p (a b)"), s_w[0])
            t_w2 = dma("sync", Wr2[:, e], I["W2"][:, e].rearrange("p a b -> p (a b)"), s_w[1])
        arena.at = qkv_at
        b1 = take(8, 8)
        t_g = [load(b1, "b1", eng="scalar")]
        assert arena.at <= qkv_at + 2048
        arena.at = base
        ii8f = take(32, 8)
        o1, o2, oo = take(32, 8), take(32, 8), take(32, 8)
        dd = take(32)
        cum, tot, pre_ = take(32, 8), take(32, 8), take(32, 8)
        cnt8, cntu, nb8, end8 = take(8), take(8, dt=u32), take(8), take(8)
        cmp_ = take(72, 8)
        sf = take(2, 32)
        eidf = take(72)
        assert arena.at <= after_a
        free = [()] * 8
        t = t_lg
        t = cp(ii8f, ii8, t)
        io = iota8.unsqueeze(1).to_broadcast([128, 32, 8])
        t2 = tt(o1, ii8f[:, :, 0:1].to_broadcast([128, 32, 8]), io, ALU.is_equal, t)
        t2 = tt(o2, ii8f[:, :, 1:2].to_broadcast([128, 32, 8]), io, ALU.is_equal, t)
        g1, g2 = g12[:, 0], g12[:, 1]
        t1 = tt(dd, mm8[:, :, 1], mm8[:, :, 0], ALU.subtract, t2)
        t1 = act(g2, dd, ACT.Exp, t1)
        t_slot, t_eid = assign(o1, o2, oo, cum, tot, pre_, cnt8, cntu, nb8, end8, cmp_, sf, eidf, t2)
        t_sc = scatter("scatter1", hall, t_slot)
        t1 = ts(g1, g2, 1.0, None, ALU.add, None, t1)
        t1 = recip(g1, g1, t1)
        t_g12 = tt(g2, g2, g1, ALU.mult, t1)
        for k in P.q:
            P.wait(k, [t_sc])
        barrier()
        arena.at = base
        Wb1, Wb2 = [take(2, 1024) for _ in range(2)], [take(8, 256) for _ in range(2)]
        assert arena.at <= after_a
        arena.at = after_a
        NX = 4
        xs = [take(256) for _ in range(NX)]
        hb = [take(2, 128) for _ in range(2)]
        hid = [take(8, 128) for _ in range(2)]
        yb = [take(256) for _ in range(NX)]
        bb1 = [take(8) for _ in range(2)]
        b2r = take(8, 256)
        assert arena.at <= after_a + 8192
        t_b2 = load(b2r, "b2")
        s_xs = [P.new_sem(f"xs{i}") for i in range(NX)]
        s_y = [P.new_sem(f"y{i}") for i in range(NX)]
        free = [()] * 8
        E = {"xs": {}, "xsr": [None] * NX, "w1": {}, "w2": {}, "w1r": [None, None], "w2r": [None, None], "br": [(), ()],
             "hb": {}, "hbr": [None, None], "hid": {}, "hidr": [None, None], "y": [None] * NX}

        def xs_load(n):
            E["xs"][n] = dma("sync", xs[n % NX], xsd[128 * n:128 * n + 128, :], s_xs[n % NX], E["xsr"][n % NX], t_sc)

        reg = {}

        def copy1(n):
            i = n % 2

            def first(e):
                reg[n] = e.value_load(eid[0:1, n:n + 1], min_val=0, max_val=7)
                return e.tensor_copy(Wb1[i].rearrange("p a b -> p (a b)").unsqueeze(1), Wr1[:, bass.ds(reg[n], 1)])
            op("vector", first, t_w1, t_eid, E["w1r"][i], *E["br"][i])
            E["w1"][n] = op("vector", lambda e: e.tensor_copy(bb1[i].unsqueeze(1), b1[:, bass.ds(reg[n], 1)]),
                            *t_g)

        def copy2(n):
            i = n % 2

            def second(e):
                r = e.value_load(eid[0:1, n:n + 1], min_val=0, max_val=7)
                return e.activation(Wb2[i].rearrange("p a b -> p (a b)").unsqueeze(1), Wr2[:, bass.ds(r, 1)], ACT.Copy)
            E["w2"][n] = op("scalar", second, t_w2, t_eid, E["w2r"][i])

        def head(n):
            i = n % 2
            for c in range(2):
                t = tr(bank(i)[:, 128 * c:128 * c + 128], xs[n % NX][:, 128 * c:128 * c + 128], E["xs"][n], *free[i],
                       sig=(c == 1))
            E["xsr"][n % NX] = t
            for c in range(2):
                E["hb"][n] = act(hb[i][:, c], bank(i)[:, 128 * c:128 * c + 128], ACT.Identity, t, E["hbr"][i],
                                 bias=lnp[:, 3, c:c + 1], scale=lnp[:, 2, c:c + 1])
            free[i] = (E["hb"][n],)

        def up(n):
            i = n % 2
            for f in range(8):
                b = 2 + 2 * i + f // 4
                o = bank(b)[:, 128 * (f % 4):128 * (f % 4) + 128]
                for k in range(2):
                    t = mm(o, Wb1[i][:, k, 128 * f:128 * f + 128], hb[i][:, k], k == 0, k == 1, E["w1"][n], E["hb"][n],
                           *free[b], sig=(k == 1))
                if f == 3:
                    for g in range(4):
                        t1 = ts(hid[i][:, g], bank(b)[:, 128 * g:128 * g + 128], bb1[i][:, g:g + 1], 0.0, ALU.add, ALU.max,
                                t, E["hidr"][i])
                    free[b] = (t1,)
                if f == 7:
                    for g in range(4):
                        t2 = act(hid[i][:, 4 + g], bank(b)[:, 128 * g:128 * g + 128], ACT.Relu, t, E["hidr"][i], E["w1"][n],
                                 bias=bb1[i][:, 4 + g:5 + g])
                    free[b] = (t2,)
            E["w1r"][i] = E["hbr"][i] = t
            E["br"][i] = (t1, t2)
            E["hid"][n] = (t1, t2)

        def down(n):
            i = n % 2
            o = bank(6 + i)[:, 0:256]
            for f in range(8):
                t = mm(o, hid[i][:, f], Wb2[i][:, f], f == 0, f == 7, *E["hid"][n], E["w2"][n], *free[6 + i], sig=(f == 7))
            E["w2r"][i] = E["hidr"][i] = t
            t = op("vector", lambda e: e.tensor_tensor(yb[n % NX].unsqueeze(1), o.unsqueeze(1), b2r[:, bass.ds(reg[n], 1)],
                                                       ALU.add), t, t_b2, E["y"][n % NX])
            free[6 + i] = (t,)
            E["y"][n % NX] = dma("sync", ysd[128 * n:128 * n + 128, :], yb[n % NX], s_y[n % NX], t)

        for n in range(3):
            xs_load(n)
        copy1(0)
        head(0)
        for n in range(NBK + 1):
            if n < NBK:
                if n + 1 < NBK:
                    head(n + 1)
                    copy1(n + 1)
                copy2(n)
                up(n)
            if n:
                down(n - 1)
            if n + 3 < NBK:
                xs_load(n + 3)
        t_ys = list(E["y"])
        arena.at = arena_m
        ya = [take(2, 256) for _ in range(32)]
        xo = [take(256) for _ in range(32)]
        s_g = [P.new_sem(f"g{i}") for i in range(8)]
        s_x2 = [P.new_sem(f"x2{i}") for i in range(8)]
        s_out = P.new_sem("out")
        t_x2 = {}
        for g in range(8):
            t_x2[g] = dma("sync", arena.t[:, arena_m + 16384 + 1024 * g:arena_m + 17408 + 1024 * g]
                          .rearrange("p (a b) -> p a b", a=4), x2d[4 * g:4 * g + 4].rearrange("m p d -> p m d"), s_x2[g],
                          E["w2"][NBK - 1])
        for g in range(8):
            for m in range(4 * g, 4 * g + 4):
                t_y = gather(ya[m], m, s_g[g], *t_ys)
            for m in range(4 * g, 4 * g + 4):
                t = stt(xo[m], ya[m][:, 0], g12[:, 0, m:m + 1], xo[m], ALU.mult, ALU.add, t_x2[g], t_y, t_g12)
                t = stt(xo[m], ya[m][:, 1], g12[:, 1, m:m + 1], xo[m], ALU.mult, ALU.add, t)
                dma("sync", out[m // 2, 128 * (m % 2):128 * (m % 2) + 128, :], xo[m], s_out, t)
        finish()


def layout(i):
    import numpy as np

    def kp(a, k):
        return np.ascontiguousarray(a.reshape(k, 128, *a.shape[1:]).swapaxes(0, 1))

    def rep(a):
        return np.ascontiguousarray(np.broadcast_to(a.reshape(1, -1), (128, a.size)))

    x = i["x"]
    cond = i["cond_1024"]
    cT = kp(np.ascontiguousarray(cond.T), 2)
    d = {
        "xT": kp(np.ascontiguousarray(x.transpose(2, 1, 0)).reshape(256, N), 2),
        "xtb": np.ascontiguousarray(x.transpose(1, 0, 2)).reshape(32, 128, 256),
        "condT": np.ascontiguousarray(np.tile(cT, (1, 1, 8))),
        "h0T": cT,
        "rW": kp(i["L0_cond_router_W"], 4),
        "rb": rep(i["L0_cond_router_bias"]),
        "w1": kp(i["L0_cond_w1"], 2), "w3": kp(i["L0_cond_w3"], 2), "w2": kp(i["L0_cond_w2"], 4),
        "W1e": np.ascontiguousarray(i["L0_cond_W1e"].reshape(8, 2, 128, 256).transpose(2, 0, 1, 3)),
        "W2e": np.ascontiguousarray(i["L0_cond_W2e"].reshape(8, 2, 128, 256).transpose(2, 0, 1, 3)),
        "gamma": np.ascontiguousarray(i["L0_ffn_gamma"].reshape(2, 128).T),
        "beta": np.ascontiguousarray(i["L0_ffn_beta"].reshape(2, 128).T),
        "wq": kp(i["L0_ffn_w_q"], 16),
        "keysT": np.ascontiguousarray(i["L0_ffn_keys"].transpose(3, 2, 0, 1).reshape(128, 16, 64)),
        "kinT": np.ascontiguousarray(i["L0_ffn_key_in"].reshape(128, 32, 2, 128).transpose(3, 2, 1, 0)),
        "kout": i["L0_ffn_key_out"].reshape(128, 32, 256),
        "Wx": kp(i["L1_cond_Wx"], 2), "Wh": kp(i["L1_cond_Wh"], 2),
        "lb": np.ascontiguousarray(i["L1_cond_b"].reshape(8, 128).T),
        "ln": np.ascontiguousarray(np.stack([i["L1_ffn_ln1_g"], i["L1_ffn_ln1_b"], i["L1_ffn_ln2_g"], i["L1_ffn_ln2_b"]])
                                   .reshape(4, 2, 128).transpose(2, 0, 1)),
        "wqkv": kp(i["L1_ffn_w_qkv"], 2),
        "bqk": np.ascontiguousarray(i["L1_ffn_b_qkv"][:512].reshape(4, 128).T),
        "bv": rep(i["L1_ffn_b_qkv"][512:]),
        "wo": kp(i["L1_ffn_w_o"], 2), "bo": rep(i["L1_ffn_b_o"]),
        "gate_w": kp(i["L1_ffn_gate_w"], 2), "gate_b": rep(i["L1_ffn_gate_b"]),
        "W1": np.ascontiguousarray(i["L1_ffn_W1"].reshape(8, 2, 128, 1024).transpose(2, 0, 1, 3)),
        "b1": np.ascontiguousarray(i["L1_ffn_b1"].reshape(8, 8, 128).transpose(2, 0, 1)),
        "W2": np.ascontiguousarray(i["L1_ffn_W2"].reshape(8, 8, 128, 256).transpose(2, 0, 1, 3)),
        "b2": rep(i["L1_ffn_b2"]).reshape(128, 8, 256),
        "ident": np.eye(128, dtype=np.float32),
        "tri": np.triu(np.ones((128, 128), np.float32), 1),
        "iota72": np.tile(np.arange(72, dtype=np.float32), (128, 1)),
        "iota8": np.tile(np.arange(8, dtype=np.float32), (128, 1)),
        "iota32": np.ascontiguousarray(np.broadcast_to(np.arange(32, dtype=np.float16)[None, :, None], (128, 32, 64))),
        "mask": (np.arange(128)[:, None] // 16 == np.arange(8)[None, :]).astype(np.float32),
    }
    return d


def kernel(**inputs):
    import numpy as np
    import concourse.bacc as bacc
    from concourse.bass_utils import run_bass_kernel_spmd

    nc = bacc.Bacc("TRN2", target_bir_lowering=False, num_devices=1)
    arrays, ins = {}, {}
    for name, a in layout({k: np.asarray(v) for k, v in inputs.items()}).items():
        a = np.ascontiguousarray(a)
        arrays[f"in_{name}"] = a
        ins[name] = nc.dram_tensor(f"in_{name}", a.shape, mybir.dt.from_np(a.dtype), kind="ExternalInput").ap()
    out = nc.dram_tensor("out_0", (NB, T, D), mybir.dt.float32, kind="ExternalOutput").ap()
    build(nc, ins, out)
    r = run_bass_kernel_spmd(nc, [arrays], core_ids=[0])
    return r.results[0]["out_0"]
```
